# Optimizing a Trainium2 kernel written in Bass

```python
import numpy as np
import jax
import jax.numpy as jnp

def _softmax(x, axis=-1):
    return jax.nn.softmax(x, axis=axis)

def _gelu(x):
    return jax.nn.gelu(x, approximate=True)

def _silu(x):
    return jax.nn.silu(x)

def _sigmoid(x):
    return jax.nn.sigmoid(x)

def _layernorm(x, axis=-1, eps=1e-05):
    m = jnp.mean(x, axis=axis, keepdims=True)
    v = jnp.var(x, axis=axis, keepdims=True)
    return (x - m) / jnp.sqrt(v + eps)

def _scatter_add(tgt, idx, src, axis=0):
    return tgt.at[idx].add(src)

def _segment_sum(src, seg, n):
    return jax.ops.segment_sum(src, seg, n)
kernel_name = 'mk_seq_postln_d2_jaxref_r4_051163'

def setup_inputs(seed: int=0):
    np.random.seed(seed)
    _w = jnp.asarray

    def _L0_attn_setup():
        import jax, jax.numpy as jnp
        import numpy as np
        D_MODEL = 512
        NHEAD = 16
        HEAD_DIM = D_MODEL // NHEAD
        LN_EPS = 1e-05
        key = jax.random.key(seed)
        ks = jax.random.split(key, 5)
        B, S, D = (4, 512, D_MODEL)
        scale = 1.0 / np.sqrt(D)
        return {'x': jax.random.normal(ks[0], (B, S, D), dtype=jnp.float32), 'Wq': jax.random.normal(ks[1], (D, D), dtype=jnp.float32) * scale, 'Wv': jax.random.normal(ks[2], (D, D), dtype=jnp.float32) * scale, 'Wg': jax.random.normal(ks[3], (D, D), dtype=jnp.float32) * scale, 'Wo': jax.random.normal(ks[4], (D, D), dtype=jnp.float32) * scale, 'beta': jnp.full((NHEAD,), -0.2, dtype=jnp.float32), 'ln_w': jnp.ones((D,), dtype=jnp.float32), 'ln_b': jnp.zeros((D,), dtype=jnp.float32)}
    _L0_attn_in = _L0_attn_setup()

    def _L0_ffn_setup():
        import jax, jax.numpy as jnp
        import numpy as np
        B, S, H, I = (1, 64, 512, 1536)

        def _quantized_matmul(x, w, scale):
            wq = w.astype(jnp.float8_e4m3fn).astype(x.dtype)
            y = jnp.einsum('bsi,io->bso', x, wq)
            return y * scale
        key = jax.random.key(seed)
        ks = jax.random.split(key, 7)
        return {'x': jax.random.normal(ks[0], (B, S, H), dtype=jnp.float32), 'gate_w': jax.random.normal(ks[1], (H, I), dtype=jnp.float32) * 0.02, 'up_w': jax.random.normal(ks[2], (H, I), dtype=jnp.float32) * 0.02, 'down_w': jax.random.normal(ks[3], (I, H), dtype=jnp.float32) * 0.02, 'gate_scale': jax.random.uniform(ks[4], (I,), dtype=jnp.float32, minval=0.5, maxval=1.5), 'up_scale': jax.random.uniform(ks[5], (I,), dtype=jnp.float32, minval=0.5, maxval=1.5), 'down_scale': jax.random.uniform(ks[6], (H,), dtype=jnp.float32, minval=0.5, maxval=1.5)}
    _L0_ffn_in = _L0_ffn_setup()

    def _L1_attn_setup():
        import jax, jax.numpy as jnp
        import numpy as np
        DIM = 512
        HEADS = 16
        HEAD_DIM = DIM // HEADS
        RANK = 16
        ALPHA = 8.0
        SCALING = ALPHA / RANK
        SCALE = HEAD_DIM ** (-0.5)

        def lora_linear(x, W, b, Bm, Am):
            out = jnp.einsum('bld,od->blo', x, W) + b
            upd = jnp.einsum('blr,or->blo', jnp.einsum('bld,rd->blr', x, Bm), Am)
            return out + SCALING * upd

        def _split(t):
            B, L, D = t.shape
            return t.reshape(B, L, HEADS, HEAD_DIM).transpose(0, 2, 1, 3)
        key = jax.random.key(seed)
        ks = jax.random.split(key, 20)
        B, L = (4, 512)
        x = jax.random.normal(ks[0], (B, L, DIM), dtype=jnp.float32)
        s = 0.02
        inp = {'x': x}
        for i, name in enumerate(['q', 'k', 'v', 'o']):
            inp[f'W{name}'] = jax.random.normal(ks[1 + 4 * i], (DIM, DIM), jnp.float32) * s
            inp[f'b{name}'] = jax.random.normal(ks[2 + 4 * i], (DIM,), jnp.float32) * s
            inp[f'B{name}'] = jax.random.normal(ks[3 + 4 * i], (RANK, DIM), jnp.float32) * s
            inp[f'A{name}'] = jax.random.uniform(ks[4 + 4 * i], (DIM, RANK), jnp.float32, -0.1, 0.1)
        return inp
    _L1_attn_in = _L1_attn_setup()

    def _L1_ffn_setup():
        import jax, jax.numpy as jnp
        import numpy as np
        EPS = 1e-08

        def _quantize(w):
            gamma = jnp.mean(jnp.abs(w))
            return jnp.clip(jnp.round(w / (gamma + EPS)), -1.0, 1.0)

        def _bitlinear(x, w):
            return jnp.matmul(x, _quantize(w).T)
        key = jax.random.key(seed)
        k1, k2, k3, k4 = jax.random.split(key, 4)
        d, h = (512, 1408)
        x = jax.random.normal(k1, (4, 512, d), dtype=jnp.float32)
        w1 = jax.random.normal(k2, (h, d), dtype=jnp.float32)
        w2 = jax.random.normal(k3, (h, d), dtype=jnp.float32)
        w3 = jax.random.normal(k4, (d, h), dtype=jnp.float32)
        return {'x': x, 'w1': w1, 'w2': w2, 'w3': w3}
    _L1_ffn_in = _L1_ffn_setup()
    _d = {'L0_attn_x': _L0_attn_in['x'], 'L0_attn_Wq': _L0_attn_in['Wq'], 'L0_attn_Wv': _L0_attn_in['Wv'], 'L0_attn_Wg': _L0_attn_in['Wg'], 'L0_attn_Wo': _L0_attn_in['Wo'], 'L0_attn_beta': _L0_attn_in['beta'], 'L0_attn_ln_w': _L0_attn_in['ln_w'], 'L0_attn_ln_b': _L0_attn_in['ln_b'], 'L0_ffn_gate_w': _L0_ffn_in['gate_w'], 'L0_ffn_up_w': _L0_ffn_in['up_w'], 'L0_ffn_down_w': _L0_ffn_in['down_w'], 'L0_ffn_gate_scale': _L0_ffn_in['gate_scale'], 'L0_ffn_up_scale': _L0_ffn_in['up_scale'], 'L0_ffn_down_scale': _L0_ffn_in['down_scale'], 'L1_attn_Wq': _L1_attn_in['Wq'], 'L1_attn_bq': _L1_attn_in['bq'], 'L1_attn_Bq': _L1_attn_in['Bq'], 'L1_attn_Aq': _L1_attn_in['Aq'], 'L1_attn_Wk': _L1_attn_in['Wk'], 'L1_attn_bk': _L1_attn_in['bk'], 'L1_attn_Bk': _L1_attn_in['Bk'], 'L1_attn_Ak': _L1_attn_in['Ak'], 'L1_attn_Wv': _L1_attn_in['Wv'], 'L1_attn_bv': _L1_attn_in['bv'], 'L1_attn_Bv': _L1_attn_in['Bv'], 'L1_attn_Av': _L1_attn_in['Av'], 'L1_attn_Wo': _L1_attn_in['Wo'], 'L1_attn_bo': _L1_attn_in['bo'], 'L1_attn_Bo': _L1_attn_in['Bo'], 'L1_attn_Ao': _L1_attn_in['Ao'], 'L1_ffn_w1': _L1_ffn_in['w1'], 'L1_ffn_w2': _L1_ffn_in['w2'], 'L1_ffn_w3': _L1_ffn_in['w3']}
    _x0 = _d['L0_attn_x']
    _d['L0_attn_x'] = jax.random.normal(jax.random.fold_in(jax.random.key(seed), 1), (4, 1024, 512), dtype=_x0.dtype)
    del _x0
    return _d

def reference(L0_attn_x, L0_attn_Wq, L0_attn_Wv, L0_attn_Wg, L0_attn_Wo, L0_attn_beta, L0_attn_ln_w, L0_attn_ln_b, L0_ffn_gate_w, L0_ffn_up_w, L0_ffn_down_w, L0_ffn_gate_scale, L0_ffn_up_scale, L0_ffn_down_scale, L1_attn_Wq, L1_attn_bq, L1_attn_Bq, L1_attn_Aq, L1_attn_Wk, L1_attn_bk, L1_attn_Bk, L1_attn_Ak, L1_attn_Wv, L1_attn_bv, L1_attn_Bv, L1_attn_Av, L1_attn_Wo, L1_attn_bo, L1_attn_Bo, L1_attn_Ao, L1_ffn_w1, L1_ffn_w2, L1_ffn_w3):

    def _L0_attn_ref(x, Wq, Wv, Wg, Wo, beta, ln_w, ln_b):
        import jax, jax.numpy as jnp
        import numpy as np
        D_MODEL = 512
        NHEAD = 16
        HEAD_DIM = D_MODEL // NHEAD
        LN_EPS = 1e-05
        B, S, D = x.shape
        H, hd = (NHEAD, HEAD_DIM)
        q = (x @ Wq.T).reshape(B, S, H, hd)
        v = (x @ Wv.T).reshape(B, S, H, hd)
        lam = jax.nn.sigmoid(beta)[None, :, None]

        def step(carry, vt):
            carry = lam * carry + vt
            return (carry, carry)
        v_t = jnp.swapaxes(v, 0, 1)
        _, st = jax.lax.scan(step, jnp.zeros((B, H, hd), dtype=v.dtype), v_t)
        state = jnp.swapaxes(st, 0, 1)
        y = (q * state).reshape(B, S, D)
        mu = jnp.mean(y, axis=-1, keepdims=True)
        var = jnp.mean(jnp.square(y - mu), axis=-1, keepdims=True)
        y = (y - mu) * jax.lax.rsqrt(var + LN_EPS) * ln_w + ln_b
        gate = jax.nn.silu(x @ Wg.T)
        y = y * gate
        return y @ Wo.T

    def _L0_ffn_ref(x, gate_w, up_w, down_w, gate_scale, up_scale, down_scale):
        import jax, jax.numpy as jnp
        import numpy as np
        B, S, H, I = (1, 64, 512, 1536)

        def _quantized_matmul(x, w, scale):
            wq = w.astype(jnp.float8_e4m3fn).astype(x.dtype)
            y = jnp.einsum('bsi,io->bso', x, wq)
            return y * scale
        gate = jax.nn.silu(_quantized_matmul(x, gate_w, gate_scale))
        up = _quantized_matmul(x, up_w, up_scale)
        fuse = gate * up
        return _quantized_matmul(fuse, down_w, down_scale)

    def _L1_attn_ref(x, Wq, bq, Bq, Aq, Wk, bk, Bk, Ak, Wv, bv, Bv, Av, Wo, bo, Bo, Ao):
        import jax, jax.numpy as jnp
        import numpy as np
        DIM = 512
        HEADS = 16
        HEAD_DIM = DIM // HEADS
        RANK = 16
        ALPHA = 8.0
        SCALING = ALPHA / RANK
        SCALE = HEAD_DIM ** (-0.5)

        def lora_linear(x, W, b, Bm, Am):
            out = jnp.einsum('bld,od->blo', x, W) + b
            upd = jnp.einsum('blr,or->blo', jnp.einsum('bld,rd->blr', x, Bm), Am)
            return out + SCALING * upd

        def _split(t):
            B, L, D = t.shape
            return t.reshape(B, L, HEADS, HEAD_DIM).transpose(0, 2, 1, 3)
        q = _split(lora_linear(x, Wq, bq, Bq, Aq))
        k = _split(lora_linear(x, Wk, bk, Bk, Ak))
        v = _split(lora_linear(x, Wv, bv, Bv, Av))
        scores = jnp.einsum('bhqd,bhkd->bhqk', q, k) * SCALE
        attn = jax.nn.softmax(scores, axis=-1)
        out = jnp.einsum('bhqk,bhkd->bhqd', attn, v)
        B, H, L, hd = out.shape
        out = out.transpose(0, 2, 1, 3).reshape(B, L, H * hd)
        return lora_linear(out, Wo, bo, Bo, Ao)

    def _L1_ffn_ref(x, w1, w2, w3):
        import jax, jax.numpy as jnp
        import numpy as np
        EPS = 1e-08

        def _quantize(w):
            gamma = jnp.mean(jnp.abs(w))
            return jnp.clip(jnp.round(w / (gamma + EPS)), -1.0, 1.0)

        def _bitlinear(x, w):
            return jnp.matmul(x, _quantize(w).T)
        x1 = _bitlinear(x, w1)
        x2 = _bitlinear(x, w2)
        hidden = jax.nn.sigmoid(x1) * x2
        return _bitlinear(hidden, w3)
    x = L0_attn_x
    x = _layernorm(x + _L0_attn_ref(x, L0_attn_Wq, L0_attn_Wv, L0_attn_Wg, L0_attn_Wo, L0_attn_beta, L0_attn_ln_w, L0_attn_ln_b), axis=-1)
    x = _layernorm(x + _L0_ffn_ref(x, L0_ffn_gate_w, L0_ffn_up_w, L0_ffn_down_w, L0_ffn_gate_scale, L0_ffn_up_scale, L0_ffn_down_scale), axis=-1)
    x = _layernorm(x + _L1_attn_ref(x, L1_attn_Wq, L1_attn_bq, L1_attn_Bq, L1_attn_Aq, L1_attn_Wk, L1_attn_bk, L1_attn_Bk, L1_attn_Ak, L1_attn_Wv, L1_attn_bv, L1_attn_Bv, L1_attn_Av, L1_attn_Wo, L1_attn_bo, L1_attn_Bo, L1_attn_Ao), axis=-1)
    x = _layernorm(x + _L1_ffn_ref(x, L1_ffn_w1, L1_ffn_w2, L1_ffn_w3), axis=-1)
    return x

_drawn_inputs = setup_inputs


def setup_inputs(seed=0):
    import zlib

    import numpy as np

    out = dict(_drawn_inputs(seed))
    spreads = {'L0_attn_beta': (-0.20000000298023224, 0.6),
     'L0_attn_ln_w': (1.0, 0.2),
     'L0_attn_ln_b': (0.0, 0.1)}
    factors = {'L1_attn_Wq': 8.0,
     'L1_attn_bq': 8.0,
     'L1_attn_Bq': 8.0,
     'L1_attn_Aq': 8.0,
     'L1_attn_Wk': 8.0,
     'L1_attn_bk': 64.0,
     'L1_attn_Bk': 8.0,
     'L1_attn_Ak': 8.0,
     'L1_attn_Wv': 3.934,
     'L1_attn_bv': 3.193,
     'L1_attn_Bv': 8.0,
     'L1_attn_Av': 8.0,
     'L1_attn_Bo': 8.0,
     'L1_attn_Ao': 8.0,
     'L1_attn_bo': 8.0}
    for name, (base, spread) in spreads.items():
        noise = np.random.default_rng([zlib.crc32(name.encode()), seed]).standard_normal(out[name].shape)
        drawn = base * np.exp(spread * noise) if base else spread * noise
        out[name] = jnp.asarray(drawn.astype(out[name].dtype))
    for name, factor in factors.items():
        out[name] = (out[name] * factor).astype(out[name].dtype)
    return out
```

```python
from contextlib import ExitStack

import numpy as np
import concourse.bass as bass
from concourse import mybir

F32 = mybir.dt.float32
F32R = mybir.dt.float32r
F16 = mybir.dt.float16
U32 = mybir.dt.uint32
ALU = mybir.AluOpType
ACT = mybir.ActivationFunctionType
AX = mybir.AxisListType

P = 128
D = 512
KT = D // P
BATCH, SEQ = 4, 1024
TOKENS = BATCH * SEQ
CHUNK = 512
CHUNKS = TOKENS // CHUNK
TT = CHUNK // P
PAIRS = CHUNKS // 2
LN_EPS = 1e-5


def need(eng, sem, value):
    if isinstance(value, int) and value <= 0:
        return
    eng.wait_ge(sem, value)


def over_pairs(eng, body):
    body(0, True, False)
    with eng.Fori(1, PAIRS - 1) as i:
        body(i, False, False)
    body(PAIRS - 1, False, True)


def tokens_of(dram, c):
    return dram[bass.ds(c * CHUNK, CHUNK), :].rearrange("(t p) d -> p t d", p=P)


def stage_semaphores(nc, stack, tag):
    taken = []

    def give_back():
        nc.clear_and_free_semaphores(taken)
        nc.all_engine_barrier()

    def sem(name):
        taken.append(nc.alloc_semaphore(name=tag + name))
        return taken[-1]

    stack.callback(give_back)
    return sem


def setup_constants(nc, ident, ones):
    with ExitStack() as stack:
        ident_cleared = stack.enter_context(nc.semaphore("ident_cleared"))
        constants_made = stack.enter_context(nc.semaphore("constants_made"))
        block = stack.enter_context(nc.Block())
        @block.gpsimd
        def _(pool):
            nc.gpsimd.memset(ident[:], 0.0).then_inc(ident_cleared, 1)
            nc.gpsimd.memset(ones[:], 1.0).then_inc(constants_made, 1)
            pool.wait_ge(ident_cleared, 1)
            nc.gpsimd.affine_select(out=ident[:], in_=ident[:], compare_op=ALU.not_equal, fill=1.0, base=0,
                                    pattern=[[-1, P]], channel_multiplier=1).then_inc(constants_made, 1)
            pool.wait_ge(constants_made, 2)


def ternary_weights(nc, ones, sources, targets):
    N = len(sources)
    shapes = [tuple(t.shape) for t in targets]
    tiles = max(s[1] for s in shapes)
    width = shapes[0][1] * shapes[0][2]
    count = P * width
    with ExitStack() as stack:
        raw = stack.enter_context(nc.sbuf_tensor("ternary_w", [P, N, width], F32))
        ratio = stack.enter_context(nc.sbuf_tensor("ternary_ratio", [P, width], F32))
        below = stack.enter_context(nc.sbuf_tensor("ternary_neg", [P, width], F16))
        sums = stack.enter_context(nc.sbuf_tensor("ternary_sums", [P, N], F32))
        gamma = stack.enter_context(nc.sbuf_tensor("ternary_gamma", [P, N], F32))
        total = stack.enter_context(nc.psum_tensor("ternary_total", [P, N], F32))
        loaded0 = stack.enter_context(nc.semaphore("ternary_loaded0"))
        loaded1 = stack.enter_context(nc.semaphore("ternary_loaded1"))
        loaded2 = stack.enter_context(nc.semaphore("ternary_loaded2"))
        summed = stack.enter_context(nc.semaphore("ternary_summed"))
        totalled = stack.enter_context(nc.semaphore("ternary_totalled"))
        gamma_made = stack.enter_context(nc.semaphore("gamma_made"))
        ratio_made = stack.enter_context(nc.semaphore("ratio_made"))
        below_made = stack.enter_context(nc.semaphore("below_made"))
        ternary_made = stack.enter_context(nc.semaphore("ternary_made"))
        block = stack.enter_context(nc.Block())
        loaded = (loaded0, loaded1, loaded2)

        @block.sync
        def _(sp):
            for n in range(N):
                view = raw[:, n, :].rearrange("p (t h) -> p t h", t=shapes[n][1])
                sp.dma_start(view, sources[n].rearrange("(t p) h -> p t h", p=P)).then_inc(loaded[n], 16)

        @block.tensor
        def _(pe):
            pe.wait_ge(summed, N)
            nc.tensor.matmul(total[:], ones[:], sums[:], start=True, stop=True).then_inc(totalled, 1)

        @block.vector
        def _(dve):
            for n in range(N):
                dve.wait_ge(loaded[n], 16)
                nc.vector.tensor_reduce(sums[:, n:n + 1], raw[:, n], AX.X, ALU.add,
                                        apply_absolute_value=True).then_inc(summed, 1)
            dve.wait_ge(totalled, 1)
            nc.vector.tensor_scalar(gamma[:], total[:], 1.0 / count, 1e-8, ALU.mult, ALU.add).then_inc(gamma_made, 1)
            dve.wait_ge(gamma_made, 1)
            nc.vector.tensor_scalar(gamma[:], gamma[:], 0.5, None, ALU.mult).then_inc(gamma_made, 1)
            dve.wait_ge(gamma_made, 2)
            nc.vector.tensor_scalar(sums[:], gamma[:], -1.0, None, ALU.mult).then_inc(gamma_made, 1)
            dve.wait_ge(gamma_made, 3)
            for n in range(N):
                if n >= 1:
                    dve.wait_ge(ternary_made, n)
                nc.vector.tensor_scalar(below[:], raw[:, n], sums[:, n:n + 1], None, ALU.is_lt).then_inc(below_made, 1)
                dve.wait_ge(below_made, n + 1)
                flat = targets[n].rearrange("p t h -> p (t h)")
                nc.vector.scalar_tensor_tensor(out=flat, in0=raw[:, n], scalar=gamma[:, n:n + 1], in1=below[:],
                                               op0=ALU.is_gt, op1=ALU.subtract).then_inc(ternary_made, 1)
            dve.wait_ge(ternary_made, N)


def fp8_weights(nc, sources, targets):
    PIECE = 2048
    pieces = []
    for source, target in zip(sources, targets):
        width = target.shape[1] * target.shape[2]
        tiles = PIECE // target.shape[2]
        for first in range(0, target.shape[1], max(tiles, 1)):
            last = min(first + max(tiles, 1), target.shape[1])
            pieces.append((source, target, first, last))
    N = len(pieces)
    with ExitStack() as stack:
        raw = stack.enter_context(nc.sbuf_tensor("fp8_raw", [P, 2, PIECE], F32))
        power = stack.enter_context(nc.sbuf_tensor("fp8_power", [P, 2, PIECE], F32))
        beyond = stack.enter_context(nc.sbuf_tensor("fp8_beyond", [P, 2, PIECE], F32))
        shifted = stack.enter_context(nc.sbuf_tensor("fp8_shifted", [P, 2, PIECE], F32))
        loaded0 = stack.enter_context(nc.semaphore("fp8_loaded0"))
        loaded1 = stack.enter_context(nc.semaphore("fp8_loaded1"))
        exponent_made = stack.enter_context(nc.semaphore("fp8_exponent_made"))
        magnitude_made = stack.enter_context(nc.semaphore("fp8_magnitude_made"))
        beyond_made = stack.enter_context(nc.semaphore("fp8_beyond_made"))
        enlarged = stack.enter_context(nc.semaphore("fp8_enlarged"))
        overflowed = stack.enter_context(nc.semaphore("fp8_overflowed"))
        addend_made = stack.enter_context(nc.semaphore("fp8_addend_made"))
        added = stack.enter_context(nc.semaphore("fp8_added"))
        rounded = stack.enter_context(nc.semaphore("fp8_rounded"))
        block = stack.enter_context(nc.Block())
        loaded = (loaded0, loaded1)

        def view(buffer, n):
            _, target, first, last = pieces[n]
            return buffer[:, n % 2, 0:(last - first) * target.shape[2]]

        @block.sync
        def _(sp):
            for n, (source, target, first, last) in enumerate(pieces):
                need(sp, rounded, n - 1)
                sp.dma_start(view(raw, n).rearrange("p (t h) -> p t h", t=last - first),
                             source.rearrange("(t p) h -> p t h", p=P)[:, first:last]).then_inc(loaded[n % 2], 16)

        @block.gpsimd
        def _(pool):
            for n in range(N):
                pool.wait_ge(exponent_made, n + 1)
                nc.gpsimd.tensor_scalar(view(power, n), view(power, n), 2.0 ** 100, 2.0 ** 19,
                                        ALU.mult, ALU.mult).then_inc(enlarged, 1)

        @block.vector
        def _(dve):
            for n, (_, target, first, last) in enumerate(pieces):
                dve.wait_ge(loaded[n % 2], 16 * (n // 2 + 1))
                need(dve, rounded, n - 1)
                nc.vector.tensor_scalar(view(power, n).bitcast(U32), view(raw, n).bitcast(U32), 0x7F800000, None,
                                        ALU.bitwise_and).then_inc(exponent_made, 1)
                nc.vector.tensor_scalar(view(beyond, n).bitcast(U32), view(raw, n).bitcast(U32), 0x7FFFFFFF, None,
                                        ALU.bitwise_and).then_inc(magnitude_made, 1)
                dve.wait_ge(magnitude_made, n + 1)
                nc.vector.tensor_scalar(view(beyond, n), view(beyond, n), 464.0, 2.0 ** 127,
                                        ALU.is_gt, ALU.mult).then_inc(beyond_made, 1)
                dve.wait_ge(enlarged, n + 1)
                dve.wait_ge(beyond_made, n + 1)
                nc.vector.tensor_tensor(view(power, n), view(beyond, n), view(power, n),
                                        ALU.add).then_inc(overflowed, 1)
                dve.wait_ge(overflowed, n + 1)
                nc.vector.tensor_scalar(view(power, n), view(power, n), 1.5 * 2.0 ** -99, 1.5 * 2.0 ** 14,
                                        ALU.mult, ALU.max).then_inc(addend_made, 1)
                dve.wait_ge(addend_made, n + 1)
                nc.vector.tensor_tensor(view(shifted, n), view(power, n), view(raw, n), ALU.subtract).then_inc(added, 1)
                dve.wait_ge(added, n + 1)
                nc.vector.tensor_tensor(target[:, first:last].rearrange("p t h -> p (t h)"), view(power, n),
                                        view(shifted, n), ALU.subtract).then_inc(rounded, 1)
            dve.wait_ge(rounded, N)


def load_scales(nc, tag, columns, rows):
    with ExitStack() as stack:
        loaded = stack.enter_context(nc.semaphore(tag + "_vectors_loaded"))
        block = stack.enter_context(nc.Block())

        @block.sync
        def _(sp):
            for source, target in columns:
                with nc.allow_non_contiguous_dma(reason="a short vector, one channel for each partition"):
                    sp.dma_start(target[:], source.rearrange("(t p) -> p t", p=P)).then_inc(loaded, 16)
            for source, target in rows:
                sp.dma_start(target[:], source.rearrange("(o n) -> o n", o=1).partition_broadcast(P)
                             ).then_inc(loaded, 16)
            sp.wait_ge(loaded, 16 * (len(columns) + len(rows)))


def split_weights(nc, tag, sources, hi, lo):
    N = len(sources)
    with ExitStack() as stack:
        raw = stack.enter_context(nc.sbuf_tensor(tag + "raw", [P, 2, KT, D], F32))
        loaded0 = stack.enter_context(nc.semaphore(tag + "loaded0"))
        loaded1 = stack.enter_context(nc.semaphore(tag + "loaded1"))
        hi_made = stack.enter_context(nc.semaphore(tag + "hi_made"))
        lo_made = stack.enter_context(nc.semaphore(tag + "lo_made"))
        block = stack.enter_context(nc.Block())
        loaded = (loaded0, loaded1)

        @block.sync
        def _(sp):
            for n in range(N):
                need(sp, lo_made, n - 1)
                sp.dma_start(raw[:, n % 2], sources[n].rearrange("(t p) h -> p t h", p=P)).then_inc(loaded[n % 2], 16)

        @block.scalar
        def _(act):
            for n in range(N):
                act.wait_ge(loaded[n % 2], 16 * (n // 2 + 1))
                nc.scalar.copy(hi[:, n], raw[:, n % 2]).then_inc(hi_made, 1)

        @block.vector
        def _(dve):
            for n in range(N):
                dve.wait_ge(hi_made, n + 1)
                nc.vector.tensor_tensor(lo[:, n], raw[:, n % 2], hi[:, n], ALU.subtract).then_inc(lo_made, 1)
            dve.wait_ge(lo_made, N)


def retention_phase(nc, x_rows, x_turned, x_out, ident, w_hi, w_lo, beta, ln_w, ln_b):
    tag = "ret_"
    WQ, WV, WG, WO = range(4)
    with ExitStack() as stack:
        def sbuf(name, shape, dtype=F32):
            return stack.enter_context(nc.sbuf_tensor(tag + name, shape, dtype))

        sem = stage_semaphores(nc, stack, tag)

        x_t = sbuf("x_t", [P, KT, CHUNK])
        x_hi = sbuf("x_hi", [P, KT, CHUNK], F32R)
        x_lo = sbuf("x_lo", [P, KT, CHUNK], F32R)
        x_tok = sbuf("x_tok", [P, 2, TT, D])
        state = sbuf("state", [P, 2, KT, CHUNK])
        q_kept = sbuf("q_kept", [P, TT, D])
        y = sbuf("y", [P, TT, D])
        gate = sbuf("gate", [P, KT, CHUNK])
        z = sbuf("z", [P, KT, CHUNK])
        z_hi = sbuf("z_hi", [P, KT, CHUNK], F32R)
        z_lo = sbuf("z_lo", [P, KT, CHUNK], F32R)
        total = sbuf("total", [P, 2, TT, D])
        decay_in = sbuf("decay_in", [P, KT])
        decay = sbuf("decay", [P, KT])
        ln_w_col = sbuf("ln_w_col", [P, KT])
        ln_b_col = sbuf("ln_b_col", [P, KT])
        minus_half = sbuf("minus_half", [P, TT])
        eps = sbuf("eps", [P, TT])
        y_stats = sbuf("y_stats", [P, TT, 6])
        y_moments = sbuf("y_moments", [P, TT, 2])
        y_var_eps = sbuf("y_var_eps", [P, TT])
        y_rstd = sbuf("y_rstd", [P, TT])
        stats = sbuf("stats", [P, TT, 6])
        moments = sbuf("moments", [P, TT, 2])
        var_eps = sbuf("var_eps", [P, TT])
        rstd = sbuf("rstd", [P, TT])
        chan_ps = stack.enter_context(nc.psum_tensor(tag + "chan_ps", [P, KT, CHUNK], F32))
        tok_ps = stack.enter_context(nc.psum_tensor(tag + "tok_ps", [P, TT, D], F32))

        vectors_loaded, decay_made, constants_set = sem("vectors_loaded"), sem("decay_made"), sem("constants_set")
        x_t_loaded, x_hi_made, x_split = sem("x_t_loaded"), sem("x_hi_made"), sem("x_split")
        x_loaded = (sem("x_loaded0"), sem("x_loaded1"))
        stored = (sem("stored0"), sem("stored1"))
        v_ready, scanned = sem("v_ready"), sem("scanned")
        q_ready, q_out = sem("q_ready"), sem("q_out")
        state_turned, y_made = sem("state_turned"), sem("y_made")
        y_stats_made, y_stats_seen, y_moments_made = sem("y_stats_made"), sem("y_stats_seen"), sem("y_moments_made")
        y_eps_added, y_rstd_made, y_normed = sem("y_eps_added"), sem("y_rstd_made"), sem("y_normed")
        y_turned, affine_made = sem("y_turned"), sem("affine_made")
        g_ready, gate_made = sem("g_ready"), sem("gate_made")
        z_made, z_hi_made, z_split = sem("z_made"), sem("z_hi_made"), sem("z_split")
        o_ready, residual = sem("o_ready"), sem("residual")
        stats_made, stats_seen, moments_made = sem("stats_made"), sem("stats_seen"), sem("moments_made")
        eps_added, rstd_made, normed = sem("eps_added"), sem("rstd_made"), sem("normed")
        block = stack.enter_context(nc.Block())

        def over_steps(eng, step, end):
            step(0, 0, 0, True)
            step(0, 1, 1, False)
            with eng.Fori(1, PAIRS) as i:
                for u in range(2):
                    step(i, 2 * i + u, u, False)
            end()

        def minus_two(i, c, u):
            return i - 1, c - 2, u

        @block.sync
        def _(sp):
            with nc.allow_non_contiguous_dma(reason="short vectors, one channel for each partition"):
                for j in range(4):
                    sp.dma_start(decay_in[32 * j:32 * j + 32, :],
                                 beta.rearrange("(k j) -> j k", j=4)[j:j + 1, :].broadcast_to([32, KT])
                                 ).then_inc(vectors_loaded, 16)
                for source, column in ((ln_w, ln_w_col), (ln_b, ln_b_col)):
                    sp.dma_start(column[:], source.rearrange("(t p) -> p t", p=P)).then_inc(vectors_loaded, 16)

            def load_turned(c):
                need(sp, x_split, c)
                sp.dma_start(x_t[:], x_turned[:, bass.ds(c * CHUNK, CHUNK)].rearrange("(t p) n -> p t n", p=P)
                             ).then_inc(x_t_loaded, 16)

            def store(c, half):
                sp.wait_ge(normed, (c + 1) * TT)
                sp.dma_start(tokens_of(x_out, c), total[:, half]).then_inc(stored[half], 16)

            def step(i, c, u, front_only):
                load_turned(c)
                need(sp, residual, (c - 1) * TT)
                sp.dma_start(x_tok[:, u], tokens_of(x_rows, c)).then_inc(x_loaded[u], 16)
                if not (isinstance(c, int) and c < 2):
                    store(c - 2, u)

            over_steps(sp, step, lambda: (store(CHUNKS - 2, 0), store(CHUNKS - 1, 1)))
            sp.wait_ge(stored[0], 16 * PAIRS)
            sp.wait_ge(stored[1], 16 * PAIRS)

        @block.gpsimd
        def _(pool):
            nc.gpsimd.memset(minus_half[:], -0.5).then_inc(constants_set, 1)
            nc.gpsimd.memset(eps[:], LN_EPS).then_inc(constants_set, 1)
            pool.wait_ge(constants_set, 2)

            def norm_scale(c, moments, moments_made, var_eps, eps_added, rstd, rstd_made, normed):
                pool.wait_ge(moments_made, (c + 1) * TT)
                need(pool, rstd_made, c)
                need(pool, normed, c * TT)
                nc.gpsimd.tensor_tensor(var_eps[:], moments[:, :, 1], eps[:], ALU.add).then_inc(eps_added, 1)
                pool.wait_ge(eps_added, c + 1)
                nc.gpsimd.tensor_tensor(rstd[:], var_eps[:], minus_half[:], ALU.pow).then_inc(rstd_made, 1)

            def result_scale(c):
                norm_scale(c, moments, moments_made, var_eps, eps_added, rstd, rstd_made, normed)

            def step(i, c, u, front_only):
                if not (isinstance(c, int) and c < 2):
                    result_scale(c - 2)
                norm_scale(c, y_moments, y_moments_made, y_var_eps, y_eps_added, y_rstd, y_rstd_made, y_normed)

            over_steps(pool, step, lambda: (result_scale(CHUNKS - 2), result_scale(CHUNKS - 1)))

        @block.scalar
        def _(act):
            act.wait_ge(vectors_loaded, 16 * 6)
            nc.scalar.activation(decay[:], decay_in[:], ACT.Sigmoid).then_inc(decay_made, 1)

            def x_high(c):
                act.wait_ge(x_t_loaded, 16 * (c + 1))
                need(act, g_ready, c * KT)
                nc.scalar.copy(x_hi[:], x_t[:]).then_inc(x_hi_made, 1)

            def keep_q(c):
                for t in range(TT):
                    act.wait_ge(q_ready, c * TT + t + 1)
                    need(act, y_made, (c - 1) * TT + t + 1)
                    nc.scalar.copy(q_kept[:, t], tok_ps[:, t]).then_inc(q_out, 1)

            def scale_and_shift(c):
                for k in range(KT):
                    act.wait_ge(y_turned, c * KT + k + 1)
                    need(act, z_split, (c - 1) * KT + k + 1)
                    nc.scalar.activation(z[:, k], chan_ps[:, k], ACT.Identity, scale=ln_w_col[:, k:k + 1],
                                         bias=ln_b_col[:, k:k + 1]).then_inc(affine_made, 1)

            def z_high(c):
                for k in range(KT):
                    act.wait_ge(z_made, c * KT + k + 1)
                    need(act, o_ready, c * TT)
                    nc.scalar.copy(z_hi[:, k], z[:, k]).then_inc(z_hi_made, 1)

            def make_gate(c):
                for k in range(KT):
                    act.wait_ge(g_ready, c * KT + k + 1)
                    need(act, z_made, (c - 1) * KT + k + 1)
                    nc.scalar.activation(gate[:, k], chan_ps[:, k], ACT.Silu).then_inc(gate_made, 1)

            def back(c):
                scale_and_shift(c)
                z_high(c)

            def step(i, c, u, front_only):
                keep_q(c)
                if not front_only:
                    back(c - 1)
                make_gate(c)
                if not (isinstance(c, int) and c == CHUNKS - 1):
                    x_high_next(c + 1)

            def x_high_next(c):
                x_high(c)

            x_high(0)
            step(0, 0, 0, True)
            step(0, 1, 1, False)
            with act.Fori(1, PAIRS - 1) as i:
                for u in range(2):
                    step(i, 2 * i + u, u, False)
            for u in range(2):
                step(PAIRS - 1, CHUNKS - 2 + u, u, False)
            back(CHUNKS - 1)

        @block.vector
        def _(dve):
            def x_low(c):
                dve.wait_ge(x_hi_made, c + 1)
                nc.vector.tensor_tensor(x_lo[:], x_t[:], x_hi[:], ALU.subtract).then_inc(x_split, 1)

            def scan(c, u):
                for k in range(KT):
                    dve.wait_ge(v_ready, c * KT + k + 1)
                    need(dve, state_turned, (c - 1) * TT)
                    if u == 1:
                        dve.wait_ge(scanned, c * KT)
                    start = 0.0 if u == 0 else state[:, 0, k, CHUNK - 1:CHUNK]
                    nc.vector.tensor_tensor_scan(state[:, u, k], decay[:, k:k + 1].to_broadcast((P, CHUNK)),
                                                 chan_ps[:, k], start, ALU.mult, ALU.add).then_inc(scanned, 1)

            def make_y(c):
                for t in range(TT):
                    dve.wait_ge(state_turned, c * TT + t + 1)
                    need(dve, y_turned, c * KT)
                    nc.vector.tensor_tensor(y[:, t], tok_ps[:, t], q_kept[:, t], ALU.mult).then_inc(y_made, 1)

            def take_y_moments(c):
                need(dve, y_moments_made, c * TT)
                for t in range(TT):
                    dve.wait_ge(y_made, c * TT + t + 1)
                    nc.vector.bn_stats(y_stats[:, t], y[:, t]).then_inc(y_stats_made, 1)
                need(dve, y_normed, c * TT)
                dve.wait_ge(y_stats_made, (c + 1) * TT)
                dve.sem_inc(y_stats_seen, 1)
                for t in range(TT):
                    nc.vector.bn_aggr(y_moments[:, t], y_stats[:, t]).then_inc(y_moments_made, 1)

            def normalise_y(c):
                dve.wait_ge(y_rstd_made, c + 1)
                for t in range(TT):
                    nc.vector.tensor_scalar(y[:, t], y[:, t], y_moments[:, t, 0:1], y_rstd[:, t:t + 1],
                                            ALU.subtract, ALU.mult).then_inc(y_normed, 1)

            def make_z(c):
                for k in range(KT):
                    dve.wait_ge(affine_made, c * KT + k + 1)
                    dve.wait_ge(gate_made, c * KT + k + 1)
                    nc.vector.tensor_tensor(z[:, k], z[:, k], gate[:, k], ALU.mult).then_inc(z_made, 1)

            def z_low(c):
                for k in range(KT):
                    dve.wait_ge(z_hi_made, c * KT + k + 1)
                    nc.vector.tensor_tensor(z_lo[:, k], z[:, k], z_hi[:, k], ALU.subtract).then_inc(z_split, 1)

            def add_residual(i, c, u):
                dve.wait_ge(x_loaded[u], 16 * (i + 1))
                need(dve, stored[u], 16 * i)
                for t in range(TT):
                    dve.wait_ge(o_ready, c * TT + t + 1)
                    nc.vector.tensor_tensor(total[:, u, t], tok_ps[:, t], x_tok[:, u, t],
                                            ALU.add).then_inc(residual, 1)

            def take_moments(c, u):
                need(dve, moments_made, c * TT)
                for t in range(TT):
                    dve.wait_ge(residual, c * TT + t + 1)
                    nc.vector.bn_stats(stats[:, t], total[:, u, t]).then_inc(stats_made, 1)
                need(dve, normed, c * TT)
                dve.wait_ge(stats_made, (c + 1) * TT)
                dve.sem_inc(stats_seen, 1)
                for t in range(TT):
                    nc.vector.bn_aggr(moments[:, t], stats[:, t]).then_inc(moments_made, 1)

            def normalise(c, u):
                dve.wait_ge(rstd_made, c + 1)
                for t in range(TT):
                    nc.vector.tensor_scalar(total[:, u, t], total[:, u, t], moments[:, t, 0:1], rstd[:, t:t + 1],
                                            ALU.subtract, ALU.mult).then_inc(normed, 1)

            def step(i, c, u, front_only):
                finishing = not (isinstance(c, int) and c < 2)
                if finishing:
                    add_residual(*minus_two(i, c, u))
                    take_moments(c - 2, u)
                scan(c, u)
                if finishing:
                    normalise(c - 2, u)
                if not front_only:
                    make_z(c - 1)
                make_y(c)
                if not front_only:
                    z_low(c - 1)
                take_y_moments(c)
                normalise_y(c)
                if not (isinstance(c, int) and c == CHUNKS - 1):
                    x_low(c + 1)

            dve.wait_ge(decay_made, 1)
            x_low(0)
            step(0, 0, 0, True)
            step(0, 1, 1, False)
            with dve.Fori(1, PAIRS - 1) as i:
                for u in range(2):
                    step(i, 2 * i + u, u, False)
            for u in range(2):
                step(PAIRS - 1, CHUNKS - 2 + u, u, False)
            add_residual(PAIRS - 1, CHUNKS - 2, 0)
            take_moments(CHUNKS - 2, 0)
            normalise(CHUNKS - 2, 0)
            make_z(CHUNKS - 1)
            z_low(CHUNKS - 1)
            add_residual(PAIRS - 1, CHUNKS - 1, 1)
            take_moments(CHUNKS - 1, 1)
            normalise(CHUNKS - 1, 1)

        @block.tensor
        def _(pe):
            PRODUCTS = ((0, 0), (0, 1), (1, 0))
            w_parts = (w_hi, w_lo)

            def to_channels(which, k_out, done):
                parts = (x_hi, x_lo)
                for k in range(KT):
                    for n, (a, b) in enumerate(PRODUCTS):
                        last = nc.tensor.matmul(chan_ps[:, k_out], w_parts[a][:, which, k, k_out * P:(k_out + 1) * P],
                                                parts[b][:, k], start=(k == 0 and n == 0),
                                                stop=(k == KT - 1 and n == 2))
                last.then_inc(done, 1)

            def to_tokens(which, parts, t, done):
                for k in range(KT):
                    for n, (a, b) in enumerate(PRODUCTS):
                        last = nc.tensor.matmul(tok_ps[:, t], parts[b][:, k, t * P:(t + 1) * P],
                                                w_parts[a][:, which, k], start=(k == 0 and n == 0),
                                                stop=(k == KT - 1 and n == 2))
                last.then_inc(done, 1)

            def turn_y(c, taken):
                pe.wait_ge(y_normed, (c + 1) * TT)
                for k in range(KT):
                    sem, per_chunk_before = taken
                    need(pe, sem, per_chunk_before * KT + k + 1)
                    for t in range(TT):
                        last = nc.tensor.transpose(chan_ps[:, k, t * P:(t + 1) * P], y[:, t, k * P:(k + 1) * P], ident)
                    last.then_inc(y_turned, 1)

            def output(c, wait):
                pe.wait_ge(z_split, (c + 1) * KT)
                for t in range(TT):
                    wait(t)
                    to_tokens(WO, (z_hi, z_lo), t, o_ready)

            def step(i, c, u, front_only):
                pe.wait_ge(x_split, c + 1)
                for k in range(KT):
                    need(pe, gate_made, (c - 1) * KT + k + 1)
                    to_channels(WV, k, v_ready)
                for t in range(TT):
                    need(pe, residual, (c - 2) * TT + t + 1)
                    to_tokens(WQ, (x_hi, x_lo), t, q_ready)
                if not front_only:
                    turn_y(c - 1, (scanned, c))
                pe.wait_ge(scanned, (c + 1) * KT)
                for t in range(TT):
                    pe.wait_ge(q_out, c * TT + t + 1)
                    for k in range(KT):
                        last = nc.tensor.transpose(tok_ps[:, t, k * P:(k + 1) * P],
                                                   state[:, u, k, t * P:(t + 1) * P], ident)
                    last.then_inc(state_turned, 1)
                for k in range(KT):
                    if front_only:
                        pe.wait_ge(scanned, (c + 1) * KT)
                    else:
                        pe.wait_ge(affine_made, (c - 1) * KT + k + 1)
                    to_channels(WG, k, g_ready)
                if not front_only:
                    output(c - 1, lambda t: pe.wait_ge(y_made, c * TT + t + 1))

            def end():
                turn_y(CHUNKS - 1, (gate_made, CHUNKS - 1))
                output(CHUNKS - 1, lambda t: pe.wait_ge(residual, (CHUNKS - 2) * TT + t + 1))

            over_steps(pe, step, end)


def ffn_phase(nc, tag, x_in, x_out, ident, w_gate, w_up, w_down, hidden_tiles,
              gate_function, gate_scale, up_scale, down_scale, hidden_type):
    HT = hidden_tiles
    RING = 4
    LAG = 3

    with ExitStack() as stack:
        x_tok = stack.enter_context(nc.sbuf_tensor(tag + "x_tok", [P, 2, TT, D], F32))
        x_hi = stack.enter_context(nc.sbuf_tensor(tag + "x_hi", [P, 2, KT, CHUNK], F16))
        x_lo = stack.enter_context(nc.sbuf_tensor(tag + "x_lo", [P, 2, KT, CHUNK], F16))
        gated = stack.enter_context(nc.sbuf_tensor(tag + "gated", [P, 2, CHUNK], F32))
        hidden = stack.enter_context(nc.sbuf_tensor(tag + "hidden", [P, 2, CHUNK], F32))
        hid_hi = stack.enter_context(nc.sbuf_tensor(tag + "hid_hi", [P, RING, CHUNK], hidden_type))
        hid_lo = stack.enter_context(nc.sbuf_tensor(tag + "hid_lo", [P, RING, CHUNK], hidden_type))
        total = stack.enter_context(nc.sbuf_tensor(tag + "total", [P, 2, TT, D], F32))
        stats = stack.enter_context(nc.sbuf_tensor(tag + "stats", [P, TT, 6], F32))
        moments = stack.enter_context(nc.sbuf_tensor(tag + "moments", [P, TT, 2], F32))
        var_eps = stack.enter_context(nc.sbuf_tensor(tag + "var_eps", [P, TT], F32))
        rstd = stack.enter_context(nc.sbuf_tensor(tag + "rstd", [P, TT], F32))
        eps = stack.enter_context(nc.sbuf_tensor(tag + "eps", [P, TT], F32))
        minus_half = stack.enter_context(nc.sbuf_tensor(tag + "minus_half", [P, TT], F32))
        gate_ps = stack.enter_context(nc.psum_tensor(tag + "gate_ps", [P, 2, CHUNK], F32))
        up_ps = stack.enter_context(nc.psum_tensor(tag + "up_ps", [P, 2, CHUNK], F32))
        down_ps = stack.enter_context(nc.psum_tensor(tag + "down_ps", [P, TT, D], F32))
        x_loaded0 = stack.enter_context(nc.semaphore(tag + "x_loaded0"))
        x_loaded1 = stack.enter_context(nc.semaphore(tag + "x_loaded1"))
        turned = stack.enter_context(nc.semaphore(tag + "turned"))
        hi_made = stack.enter_context(nc.semaphore(tag + "hi_made"))
        split = stack.enter_context(nc.semaphore(tag + "split"))
        projected = stack.enter_context(nc.semaphore(tag + "projected"))
        gate_made = stack.enter_context(nc.semaphore(tag + "gate_made"))
        hidden_made = stack.enter_context(nc.semaphore(tag + "hidden_made"))
        hid_hi_made = stack.enter_context(nc.semaphore(tag + "hid_hi_made"))
        hid_lo_made = stack.enter_context(nc.semaphore(tag + "hid_lo_made"))
        hid_used = stack.enter_context(nc.semaphore(tag + "hid_used"))
        drained = stack.enter_context(nc.semaphore(tag + "drained"))
        residual = stack.enter_context(nc.semaphore(tag + "residual"))
        stats_made = stack.enter_context(nc.semaphore(tag + "stats_made"))
        stats_seen = stack.enter_context(nc.semaphore(tag + "stats_seen"))
        moments_made = stack.enter_context(nc.semaphore(tag + "moments_made"))
        half_set = stack.enter_context(nc.semaphore(tag + "half_set"))
        eps_added = stack.enter_context(nc.semaphore(tag + "eps_added"))
        rstd_made = stack.enter_context(nc.semaphore(tag + "rstd_made"))
        normed = stack.enter_context(nc.semaphore(tag + "normed"))
        stored0 = stack.enter_context(nc.semaphore(tag + "stored0"))
        stored1 = stack.enter_context(nc.semaphore(tag + "stored1"))
        block = stack.enter_context(nc.Block())
        x_loaded = (x_loaded0, x_loaded1)
        stored = (stored0, stored1)

        def slot(u, j):
            return (u * (HT + 2) + 2 + j) % 2

        def turn_bank(u, k):
            ring = gate_ps if k % 2 == 0 else up_ps
            return ring[:, slot(u, k // 2 - 2), :]

        def slot_user(n, j):
            if j >= RING:
                return n - RING + 1
            before = j + RING * ((HT - 1 - j) // RING)
            return n - j - HT + before + 1

        @block.sync
        def _(sp):
            def pair(i, first, last):
                for u in range(2):
                    c = 2 * i + u
                    need(sp, residual, (c - 1) * TT)
                    sp.dma_start(x_tok[:, u], tokens_of(x_in, c)).then_inc(x_loaded[u], 16)
                    if not (first and u == 0):
                        sp.wait_ge(normed, c * TT)
                        sp.dma_start(tokens_of(x_out, c - 1), total[:, 1 - u]).then_inc(stored[1 - u], 16)
            over_pairs(sp, pair)
            sp.wait_ge(normed, CHUNKS * TT)
            sp.dma_start(tokens_of(x_out, CHUNKS - 1), total[:, 1]).then_inc(stored1, 16)
            sp.wait_ge(stored0, 16 * PAIRS)
            sp.wait_ge(stored1, 16 * PAIRS)

        @block.gpsimd
        def _(pool):
            nc.gpsimd.memset(minus_half[:], -0.5).then_inc(half_set, 1)
            nc.gpsimd.memset(eps[:], LN_EPS).then_inc(half_set, 1)
            pool.wait_ge(half_set, 2)

            def norm_scale(c):
                pool.wait_ge(moments_made, (c + 1) * TT)
                need(pool, rstd_made, c)
                need(pool, normed, c * TT)
                nc.gpsimd.tensor_tensor(var_eps[:], moments[:, :, 1], eps[:], ALU.add).then_inc(eps_added, 1)
                pool.wait_ge(eps_added, c + 1)
                nc.gpsimd.tensor_tensor(rstd[:], var_eps[:], minus_half[:], ALU.pow).then_inc(rstd_made, 1)

            over_pairs(pool, lambda i, first, last: (norm_scale(2 * i), norm_scale(2 * i + 1)))

        @block.scalar
        def _(act):
            def high_parts(c, u):
                for k in range(KT):
                    act.wait_ge(turned, c * KT + k + 1)
                    if k == 0:
                        need(act, projected, (c - 1) * HT)
                    nc.scalar.copy(x_hi[:, u, k], turn_bank(u, k)).then_inc(hi_made, 1)

            def hidden_high(c, u, j):
                n = c * HT + j
                act.wait_ge(hidden_made, n + 1)
                need(act, hid_used, slot_user(n, j))
                nc.scalar.copy(hid_hi[:, j % RING], hidden[:, (u * HT + j) % 2]).then_inc(hid_hi_made, 1)

            def pair(i, first, last):
                for u in range(2):
                    c = 2 * i + u
                    for j in range(HT):
                        n = c * HT + j
                        act.wait_ge(projected, n + 1)
                        need(act, hidden_made, n - 1)
                        scale = 1.0 if gate_scale is None else gate_scale[:, j:j + 1]
                        nc.scalar.activation(gated[:, (u * HT + j) % 2], gate_ps[:, slot(u, j)],
                                             gate_function, scale=scale).then_inc(gate_made, 1)
                        if j >= 1:
                            hidden_high(c, u, j - 1)
                    hidden_high(c, u, HT - 1)
                    if not (last and u == 1):
                        high_parts(c + 1, 1 - u)

            high_parts(0, 0)
            over_pairs(act, pair)

        @block.vector
        def _(dve):
            def low_parts(c, u):
                for k in range(KT):
                    dve.wait_ge(hi_made, c * KT + k + 1)
                    nc.vector.tensor_tensor(x_lo[:, u, k], turn_bank(u, k), x_hi[:, u, k],
                                            ALU.subtract).then_inc(split, 1)

            def hidden_low(c, u, j):
                dve.wait_ge(hid_hi_made, c * HT + j + 1)
                nc.vector.tensor_tensor(hid_lo[:, j % RING], hidden[:, (u * HT + j) % 2],
                                        hid_hi[:, j % RING], ALU.subtract).then_inc(hid_lo_made, 1)

            def drain(i, c, u):
                dve.wait_ge(hid_used, (c + 1) * HT)
                need(dve, stored[u], 16 * i)
                for t in range(TT):
                    if down_scale is None:
                        if t == 0:
                            dve.wait_ge(x_loaded[u], 16 * (i + 1))
                        nc.vector.tensor_tensor(total[:, u, t], down_ps[:, t], x_tok[:, u, t],
                                                ALU.add).then_inc(residual, 1)
                    else:
                        nc.vector.tensor_tensor(total[:, u, t], down_ps[:, t], down_scale,
                                                ALU.mult).then_inc(drained, 1)

            def add_input(i, c, u):
                if down_scale is None:
                    return
                dve.wait_ge(x_loaded[u], 16 * (i + 1))
                for t in range(TT):
                    dve.wait_ge(drained, c * TT + t + 1)
                    nc.vector.tensor_tensor(total[:, u, t], total[:, u, t], x_tok[:, u, t],
                                            ALU.add).then_inc(residual, 1)

            def take_stats(c, u):
                need(dve, moments_made, c * TT)
                for t in range(TT):
                    dve.wait_ge(residual, c * TT + t + 1)
                    nc.vector.bn_stats(stats[:, t], total[:, u, t]).then_inc(stats_made, 1)

            def take_moments(c):
                need(dve, normed, c * TT)
                dve.wait_ge(stats_made, (c + 1) * TT)
                dve.sem_inc(stats_seen, 1)
                for t in range(TT):
                    nc.vector.bn_aggr(moments[:, t], stats[:, t]).then_inc(moments_made, 1)

            def normalise(c, u):
                dve.wait_ge(rstd_made, c + 1)
                for t in range(TT):
                    nc.vector.tensor_scalar(total[:, u, t], total[:, u, t], moments[:, t, 0:1], rstd[:, t:t + 1],
                                            ALU.subtract, ALU.mult).then_inc(normed, 1)

            def finish(i, c, u, step):
                if step == 0:
                    drain(i, c, u)
                elif step == 1:
                    add_input(i, c, u)
                elif step == 2:
                    take_stats(c, u)
                elif step == 3:
                    take_moments(c)
                elif step == 6:
                    normalise(c, u)

            def pair(i, first, last):
                for u in range(2):
                    c = 2 * i + u
                    for j in range(HT):
                        if not (first and u == 0):
                            finish(i - 1 + u, c - 1, 1 - u, j)
                        n = c * HT + j
                        dve.wait_ge(gate_made, n + 1)
                        need(dve, hid_lo_made, n - 1)
                        m = (u * HT + j) % 2
                        if up_scale is None:
                            nc.vector.tensor_tensor(hidden[:, m], up_ps[:, slot(u, j)], gated[:, m],
                                                    ALU.mult).then_inc(hidden_made, 1)
                        else:
                            nc.vector.scalar_tensor_tensor(
                                out=hidden[:, m], in0=up_ps[:, slot(u, j)], scalar=up_scale[:, j:j + 1],
                                in1=gated[:, m], op0=ALU.mult, op1=ALU.mult).then_inc(hidden_made, 1)
                        if j >= 1:
                            hidden_low(c, u, j - 1)
                    hidden_low(c, u, HT - 1)
                    if not (last and u == 1):
                        low_parts(c + 1, 1 - u)

            low_parts(0, 0)
            over_pairs(dve, pair)
            for step in range(7):
                finish(PAIRS - 1, CHUNKS - 1, 1, step)

        @block.tensor
        def _(pe):
            def turn(i, c, u):
                pe.wait_ge(x_loaded[u], 16 * (i + 1))
                for k in range(KT):
                    need(pe, gate_made if k % 2 == 0 else hidden_made, (c - 1) * HT + HT - 1 + k // 2)
                    for t in range(TT):
                        last = nc.tensor.transpose(turn_bank(u, k)[:, t * P:(t + 1) * P],
                                                   x_tok[:, u, t, k * P:(k + 1) * P], ident)
                    last.then_inc(turned, 1)

            def project(c, u, j):
                n = c * HT + j
                if j == 0:
                    pe.wait_ge(split, (c + 1) * KT)
                for weight, bank, taken in ((w_gate, gate_ps, gate_made), (w_up, up_ps, hidden_made)):
                    if j >= 2:
                        pe.wait_ge(taken, n - 1)
                    for k in range(KT):
                        for part in (x_hi, x_lo):
                            last = nc.tensor.matmul(bank[:, slot(u, j)], weight[:, k, j * P:(j + 1) * P],
                                                    part[:, u, k], start=(k == 0 and part is x_hi),
                                                    stop=(k == KT - 1 and part is x_lo))
                last.then_inc(projected, 1)

            def down(c, j):
                pe.wait_ge(hid_lo_made, c * HT + j + 1)
                for t in range(TT):
                    if j == 0:
                        need(pe, residual if down_scale is None else drained, (c - 1) * TT + t + 1)
                    for part in (hid_hi, hid_lo):
                        last = nc.tensor.matmul(down_ps[:, t], part[:, j % RING, t * P:(t + 1) * P], w_down[:, j],
                                                start=(j == 0 and part is hid_hi),
                                                stop=(j == HT - 1 and part is hid_lo))
                last.then_inc(hid_used, 1)

            def pair(i, first, last):
                for u in range(2):
                    c = 2 * i + u
                    for j in range(HT):
                        project(c, u, j)
                        if j >= LAG:
                            down(c, j - LAG)
                    if not (last and u == 1):
                        turn(i + u, c + 1, 1 - u)
                    for j in range(HT - LAG, HT):
                        down(c, j)

            turn(0, 0, 0)
            over_pairs(pe, pair)


HEADS = 16
HEAD = D // HEADS
RANK = 16
LORA_SCALE = 8.0 / RANK
SOFTMAX_SCALE = HEAD ** -0.5
WEIGHT_LIFT = 256.0
QUERY_LIFT = 32.0
MAX_LIFT = 2.0 ** 14


def lora_weights(nc, weights, a_turned, b_rows, biases, w_hi, w_lo, bias_cols, bias_rows, exp_scale, out_scale):
    tag = "lora_"
    Q, K, V, O = range(4)
    with ExitStack() as stack:
        def sbuf(name, shape, dtype=F32):
            return stack.enter_context(nc.sbuf_tensor(tag + name, shape, dtype))

        def sem(name):
            return stack.enter_context(nc.semaphore(tag + name))

        raw = sbuf("raw", [P, 4, KT, D])
        a_sb = sbuf("a_sb", [RANK, 4, D])
        b_sb = sbuf("b_sb", [RANK, 4, D])
        ident = sbuf("ident", [P, P])
        largest = sbuf("largest", [P, 2, 4])
        both = sbuf("both", [P, 4])
        top = sbuf("top", [4, 1])
        top_row = sbuf("top_row", [4, P])
        zeros = sbuf("zeros", [4, P])
        power = sbuf("power", [P, 4])
        inverse = sbuf("inverse", [P, 4])
        lift = sbuf("lift", [P, 4])
        update = stack.enter_context(nc.psum_tensor(tag + "update", [P, KT, D], F32))
        turned = stack.enter_context(nc.psum_tensor(tag + "turned", [4, P], F32))
        spread = stack.enter_context(nc.psum_tensor(tag + "spread", [P, 4], F32))
        loaded = [sem("loaded%d" % n) for n in range(4)]
        vectors_loaded, ident_made, chain = sem("vectors_loaded"), sem("ident_made"), sem("chain")
        updated, added, maxed, max_turned, top_made = (sem("updated"), sem("added"), sem("maxed"),
                                                       sem("max_turned"), sem("top_made"))
        top_spread, lift_made, hi_made, lo_made = sem("top_spread"), sem("lift_made"), sem("hi_made"), sem("lo_made")
        block = stack.enter_context(nc.Block())

        @block.sync
        def _(sp):
            for n in range(4):
                sp.dma_start(a_sb[:, n], a_turned[n]).then_inc(loaded[n], 16)
                sp.dma_start(b_sb[:, n], b_rows[n]).then_inc(loaded[n], 16)
                sp.dma_start(raw[:, n], weights[n].rearrange("(t p) h -> p t h", p=P)).then_inc(loaded[n], 16)
            with nc.allow_non_contiguous_dma(reason="short vectors, one channel for each partition"):
                for n in (Q, K):
                    sp.dma_start(bias_cols[:, n], biases[n].rearrange("(t p) -> p t", p=P)).then_inc(vectors_loaded, 16)
            for n in (V, O):
                sp.dma_start(bias_rows[:, n - V], biases[n].rearrange("(o n) -> o n", o=1).partition_broadcast(P)
                             ).then_inc(vectors_loaded, 16)

        @block.gpsimd
        def _(pool):
            nc.gpsimd.memset(zeros[:], 0.0).then_inc(ident_made, 1)
            nc.gpsimd.memset(ident[:], 0.0).then_inc(ident_made, 1)
            pool.wait_ge(ident_made, 2)
            nc.gpsimd.affine_select(out=ident[:], in_=ident[:], compare_op=ALU.not_equal, fill=1.0, base=0,
                                    pattern=[[-1, P]], channel_multiplier=1).then_inc(ident_made, 1)

        @block.tensor
        def _(pe):
            for n in range(4):
                pe.wait_ge(loaded[n], 48)
                need(pe, added, n)
                for k in range(KT):
                    last = nc.tensor.matmul(update[:, k], b_sb[:, n, k * P:(k + 1) * P], a_sb[:, n],
                                            start=True, stop=True)
                last.then_inc(updated, 1)
            pe.wait_ge(ident_made, 3)
            pe.wait_ge(maxed, 9)
            nc.tensor.transpose(turned[:], both[:], ident[:]).then_inc(max_turned, 1)
            pe.wait_ge(top_made, 2)
            nc.tensor.matmul(spread[:], top_row[:], ident[0:4, 0:4], start=True, stop=True).then_inc(top_spread, 1)

        @block.scalar
        def _(act):
            act.wait_ge(lift_made, 1)
            for n in range(4):
                nc.scalar.activation(w_hi[:, n], raw[:, n], ACT.Copy, scale=lift[:, n:n + 1]).then_inc(hi_made, 1)

        @block.vector
        def _(dve):
            for n in range(4):
                dve.wait_ge(updated, n + 1)
                nc.vector.scalar_tensor_tensor(
                    out=raw[:, n].rearrange("p t h -> p (t h)"), in0=update[:].rearrange("p t h -> p (t h)"),
                    scalar=LORA_SCALE, in1=raw[:, n].rearrange("p t h -> p (t h)"),
                    op0=ALU.mult, op1=ALU.add).then_inc(added, 1)
                dve.wait_ge(added, n + 1)
                nc.vector.tensor_reduce(largest[:, 0, n:n + 1], raw[:, n], AX.XY, ALU.max,
                                        apply_absolute_value=True).then_inc(maxed, 1)
            dve.wait_ge(vectors_loaded, 64)
            for n in range(4):
                bias = bias_cols[:, n] if n < V else bias_rows[:, n - V]
                nc.vector.tensor_reduce(largest[:, 1, n:n + 1], bias, AX.X, ALU.max,
                                        apply_absolute_value=True).then_inc(maxed, 1)
            dve.wait_ge(maxed, 8)
            nc.vector.tensor_tensor(both[:], largest[:, 0], largest[:, 1], ALU.max).then_inc(maxed, 1)
            dve.wait_ge(max_turned, 1)
            nc.vector.tensor_reduce(top[:], turned[:], AX.X, ALU.max).then_inc(top_made, 1)
            dve.wait_ge(top_made, 1)
            dve.wait_ge(ident_made, 3)
            nc.vector.tensor_scalar(top_row[:], zeros[:], top[:, 0:1], None, ALU.add).then_inc(top_made, 1)
            dve.wait_ge(top_spread, 1)
            nc.vector.tensor_scalar(power[:], spread[:], 2.0 ** -101, None, ALU.max).then_inc(chain, 1)
            dve.wait_ge(chain, 1)
            nc.vector.tensor_scalar(power[:].bitcast(U32), power[:].bitcast(U32), 0x7F800000, None,
                                    ALU.bitwise_and).then_inc(chain, 1)
            dve.wait_ge(chain, 2)
            nc.vector.tensor_scalar(power[:], power[:], 2.0, None, ALU.mult).then_inc(chain, 1)
            dve.wait_ge(chain, 3)
            nc.vector.reciprocal(inverse[:], power[:]).then_inc(chain, 1)
            dve.wait_ge(chain, 4)
            nc.vector.tensor_scalar(lift[:], inverse[:], WEIGHT_LIFT, None, ALU.mult).then_inc(lift_made, 1)
            nc.vector.tensor_scalar(bias_cols[:, Q], bias_cols[:, Q], inverse[:, Q:Q + 1], QUERY_LIFT,
                                    ALU.mult, ALU.mult).then_inc(chain, 1)
            nc.vector.tensor_scalar(bias_cols[:, K], bias_cols[:, K], inverse[:, K:K + 1], None,
                                    ALU.mult).then_inc(chain, 1)
            nc.vector.tensor_scalar(bias_rows[:, 0], bias_rows[:, 0], inverse[:, V:V + 1], None,
                                    ALU.mult).then_inc(chain, 1)
            nc.vector.tensor_scalar(exp_scale[:], power[:, Q:Q + 1], power[:, K:K + 1], SOFTMAX_SCALE / QUERY_LIFT,
                                    ALU.mult, ALU.mult).then_inc(chain, 1)
            nc.vector.tensor_scalar(out_scale[:], power[:, V:V + 1], power[:, O:O + 1],
                                    1.0 / (QUERY_LIFT * WEIGHT_LIFT), ALU.mult, ALU.mult).then_inc(chain, 1)
            dve.wait_ge(lift_made, 1)
            for n in range(4):
                dve.wait_ge(hi_made, n + 1)
                flat = "p t h -> p (t h)"
                nc.vector.scalar_tensor_tensor(out=w_lo[:, n].rearrange(flat), in0=raw[:, n].rearrange(flat),
                                               scalar=lift[:, n:n + 1], in1=w_hi[:, n].rearrange(flat),
                                               op0=ALU.mult, op1=ALU.subtract).then_inc(lo_made, 1)
            dve.wait_ge(lo_made, 4)
            dve.wait_ge(chain, 9)


def attention_phase(nc, x_in, x_out, ident, ones, w_hi, w_lo, bias_cols, bias_rows, exp_scale, out_scale):
    tag = "att_"
    WQ, WK, WV, WO = range(4)
    GROUPS = KT
    STEPS = BATCH * GROUPS
    G_HEADS = P // HEAD
    KEY_TILES = SEQ // P
    HALVES = SEQ // CHUNK
    PAIR = 2
    UNITS = HALVES * KEY_TILES * G_HEADS // PAIR
    HALF_UNITS = UNITS // HALVES
    MAXES = G_HEADS * KEY_TILES * HALVES
    ROWS = 3 * HEAD + 1
    PROBS = 4
    POOLED = 4
    TILES = SEQ // P
    STACK_DMAS = 6 * G_HEADS
    NORM_UNITS = (10, 14)

    with ExitStack() as stack:
        def sbuf(name, shape, dtype=F32):
            return stack.enter_context(nc.sbuf_tensor(tag + name, shape, dtype))

        def psum(name, shape):
            return stack.enter_context(nc.psum_tensor(tag + name, shape, F32))

        def sem(name):
            return stack.enter_context(nc.semaphore(tag + name))

        x_tok = sbuf("x_tok", [P, 2, TT, D])
        x_hi = sbuf("x_hi", [P, KT, SEQ], F16)
        x_lo = sbuf("x_lo", [P, KT, SEQ], F16)
        v = sbuf("v", [P, KEY_TILES, D])
        queries = sbuf("queries", [ROWS, 2, G_HEADS, SEQ], F16)
        keys = sbuf("keys", [ROWS, 2, G_HEADS, SEQ], F16)
        qk_full = sbuf("qk_full", [P, 2, CHUNK])
        qk_hi = sbuf("qk_hi", [P, 2, SEQ], F16)
        qk_lo = sbuf("qk_lo", [P, 2, SEQ], F16)
        maxes = sbuf("maxes", [P, MAXES // HALVES, HALVES])
        row_max = sbuf("row_max", [P, MAXES // HALVES])
        max_rows = sbuf("max_rows", [MAXES // HALVES, P], F16)
        probs = sbuf("probs", [P, PROBS, PAIR, CHUNK])
        prob_sums = sbuf("prob_sums", [P, G_HEADS, CHUNK])
        mixed = sbuf("mixed", [P, 2, CHUNK])
        recip = sbuf("recip", [P, 2, CHUNK])
        z = sbuf("z", [P, 2, CHUNK])
        z_hi = sbuf("z_hi", [P, GROUPS, SEQ], F16)
        z_lo = sbuf("z_lo", [P, GROUPS, SEQ], F16)
        total = sbuf("total", [P, 2, TT, D])
        stats = sbuf("stats", [P, TT, 6])
        moments = sbuf("moments", [P, TT, 2])
        var_eps = sbuf("var_eps", [P, TT])
        rstd = sbuf("rstd", [P, TT])
        minus_half = sbuf("minus_half", [P, TT])
        eps = sbuf("eps", [P, TT])
        score_ps = psum("score_ps", [P, 2, PAIR, CHUNK])
        aux_ps = psum("aux_ps", [P, 2, CHUNK])
        mix_ps = psum("mix_ps", [P, CHUNK])
        sum_ps = psum("sum_ps", [P, CHUNK])

        constants_set, key_ones_set = sem("constants_set"), sem("key_ones_set")
        rows_loaded = (sem("rows_loaded0"), sem("rows_loaded1"))
        skip_loaded = (sem("skip_loaded0"), sem("skip_loaded1"))
        stored = (sem("stored0"), sem("stored1"))
        x_turned, x_hi_made, x_split = sem("x_turned"), sem("x_hi_made"), sem("x_split")
        v_ready, v_made = sem("v_ready"), sem("v_made")
        qk_ready, qk_full_made, qk_hi_made, qk_split = (sem("qk_ready"), sem("qk_full_made"), sem("qk_hi_made"),
                                                        sem("qk_split"))
        buffer_seen = sem("buffer_seen")
        stacked = (sem("stacked0"), sem("stacked1"))
        m_ready, maxed, row_max_made = sem("m_ready"), sem("maxed"), sem("row_max_made")
        rows_turned, rows_made, rows_stacked = sem("rows_turned"), sem("rows_made"), sem("rows_stacked")
        scored, exp_made, pooled, weighed = sem("scored"), sem("exp_made"), sem("pooled"), sem("weighed")
        mix_kept, recip_made, z_made, z_hi_made, z_split = (sem("mix_kept"), sem("recip_made"), sem("z_made"),
                                                            sem("z_hi_made"), sem("z_split"))
        o_ready, skipped, residual = sem("o_ready"), sem("skipped"), sem("residual")
        stats_made, stats_seen, moments_made = sem("stats_made"), sem("stats_seen"), sem("moments_made")
        eps_added, rstd_made, normed = sem("eps_added"), sem("rstd_made"), sem("normed")
        block = stack.enter_context(nc.Block())

        def is_last(b):
            return isinstance(b, int) and b == BATCH - 1

        def is_first(b):
            return isinstance(b, int) and b == 0

        def over_batches(eng, body):
            body(0)
            with eng.Fori(1, BATCH - 1) as b:
                body(b)
            body(BATCH - 1)

        def unit_work(b, g):
            work = {e: [] for e in range(UNITS)}
            if g == 0:
                work[1] += [("v", t) for t in range(TILES)]
                if not is_first(b):
                    for t in range(TILES):
                        work[5 + t // 2].append(("o", t))
            if g == 2 and not is_last(b):
                for t in range(2 * KT):
                    work[1 + t // 2].append(("t", t))
            if not (is_last(b) and g >= GROUPS - 2):
                for t in range(4):
                    work[HALF_UNITS + 2 + t].append(("q", t))
            if not (is_last(b) and g == GROUPS - 1):
                first = list(range(8, HALF_UNITS + 2)) + list(range(HALF_UNITS + 6, UNITS - 1))
                for m in range(MAXES):
                    work[first[m * len(first) // MAXES]].append(("m", m))
            return work

        @block.sync
        def _(sp):
            def load_rows(b, u):
                need(sp, x_turned, b * 2 * KT)
                need(sp, skipped, (b - 2) * TILES + (u + 1) * TT)
                sp.dma_start(x_tok[:, u], tokens_of(x_in, b * HALVES + u)).then_inc(rows_loaded[u], 16)

            def load_skip(b, u):
                if is_last(b):
                    sp.wait_ge(skipped, (b - 1) * TILES + (u + 1) * TT)
                else:
                    sp.wait_ge(x_turned, (b + 2) * 2 * KT)
                sp.dma_start(x_tok[:, u], tokens_of(x_in, b * HALVES + u)).then_inc(skip_loaded[u], 16)

            def stack_step(n, buffer):
                need(sp, scored, (n - 1) * UNITS)
                sp.sem_inc(buffer_seen, 1)
                for which, target, parts in ((0, queries, (qk_hi, qk_lo, qk_hi)), (1, keys, (qk_hi, qk_hi, qk_lo))):
                    sp.wait_ge(qk_split, 4 * n + 2 * which + 2)
                    for row, part in enumerate(parts):
                        for j in range(G_HEADS):
                            sp.dma_start(target[row * HEAD:(row + 1) * HEAD, buffer, j, :],
                                         part[j * HEAD:(j + 1) * HEAD, which, :]).then_inc(stacked[buffer], 16)

            def stack_max(n, buffer):
                sp.wait_ge(rows_made, n + 1)
                sp.dma_start(queries[3 * HEAD:ROWS, buffer].rearrange("o j (t p) -> o (j t) p", p=P),
                             max_rows[:, :]).then_inc(rows_stacked, 16)

            def store(b, u):
                sp.wait_ge(normed, b * TILES + (u + 1) * TT)
                sp.dma_start(tokens_of(x_out, b * HALVES + u), total[:, u]).then_inc(stored[u], 16)

            for u in range(HALVES):
                sp.sem_inc(stored[u], 16)
                load_rows(0, u)
            stack_step(0, 0)
            stack_step(1, 1)
            stack_max(0, 0)

            def body(b):
                for g in range(GROUPS):
                    n = b * GROUPS + g
                    if g == 0 and not is_first(b):
                        for u in range(HALVES):
                            load_skip(b - 1, u)
                    if not (is_first(b) and g == 0) and not (is_last(b) and g == GROUPS - 1):
                        stack_step(n + 1, (g + 1) % 2)
                    if g == 0 and not is_first(b):
                        for u in range(HALVES):
                            store(b - 1, u)
                    if g == 1 and not is_last(b):
                        for u in range(HALVES):
                            load_rows(b + 1, u)
                    if not (is_last(b) and g == GROUPS - 1):
                        stack_max(n + 1, (g + 1) % 2)

            over_batches(sp, body)
            for u in range(HALVES):
                load_skip(BATCH - 1, u)
            for u in range(HALVES):
                store(BATCH - 1, u)
                sp.wait_ge(stored[u], 16 * (BATCH + 1))

        @block.gpsimd
        def _(pool):
            nc.gpsimd.memset(minus_half[:], -0.5).then_inc(constants_set, 1)
            nc.gpsimd.memset(eps[:], LN_EPS).then_inc(constants_set, 1)
            pool.wait_ge(constants_set, 2)

            def qk_low(n, t):
                pool.wait_ge(qk_hi_made, 4 * n + t + 1)
                which, half = t // 2, t % 2
                nc.gpsimd.tensor_tensor(qk_lo[:, which, half * CHUNK:(half + 1) * CHUNK], qk_full[:, t % 2],
                                        qk_hi[:, which, half * CHUNK:(half + 1) * CHUNK],
                                        ALU.subtract).then_inc(qk_split, 1)

            def sum_probs(n, unit):
                kt, pair = (unit % HALF_UNITS) // 2, unit % 2
                half = n * HALVES + unit // HALF_UNITS
                sums = prob_sums[:, PAIR * pair:PAIR * pair + PAIR]
                pool.wait_ge(exp_made, n * UNITS + unit + 1)
                if kt == 1:
                    need(pool, weighed, half * KEY_TILES - KEY_TILES + POOLED + 1)
                    nc.gpsimd.tensor_tensor(sums, probs[:, (unit - 2) % PROBS], probs[:, unit % PROBS],
                                            ALU.add).then_inc(pooled, 1)
                else:
                    pool.wait_ge(pooled, half * 2 * (POOLED - 1) + 2 * (kt - 2) + pair + 1)
                    nc.gpsimd.tensor_tensor(sums, sums, probs[:, unit % PROBS], ALU.add).then_inc(pooled, 1)

            def z_low(n, half, g):
                pool.wait_ge(z_hi_made, n * HALVES + half + 1)
                at = slice(half * CHUNK, (half + 1) * CHUNK)
                nc.gpsimd.tensor_tensor(z_lo[:, g, at], z[:, half], z_hi[:, g, at], ALU.subtract).then_inc(z_split, 1)

            def norm_scale(c):
                pool.wait_ge(moments_made, (c + 1) * TT)
                nc.gpsimd.tensor_tensor(var_eps[:], moments[:, :, 1], eps[:], ALU.add).then_inc(eps_added, 1)
                pool.wait_ge(eps_added, c + 1)
                nc.gpsimd.tensor_tensor(rstd[:], var_eps[:], minus_half[:], ALU.pow).then_inc(rstd_made, 1)

            for n in range(2):
                for t in range(4):
                    qk_low(n, t)

            def body(b):
                for g in range(GROUPS):
                    n = b * GROUPS + g
                    work = unit_work(b, g)
                    for unit in range(UNITS):
                        if unit == 5 and not (is_first(b) and g == 0):
                            z_low(n - 1, 1, (g - 1) % GROUPS)
                        if unit == HALF_UNITS + 6:
                            z_low(n, 0, g)
                        kt = (unit % HALF_UNITS) // 2
                        if 1 <= kt < POOLED:
                            sum_probs(n, unit)
                        for kind, t in work[unit]:
                            if kind == "q":
                                qk_low(n + 2, t)
                        if g == 0 and not is_first(b) and unit in (NORM_UNITS[0], NORM_UNITS[1]):
                            norm_scale((b - 1) * HALVES + NORM_UNITS.index(unit))

            over_batches(pool, body)
            z_low(STEPS - 1, 1, GROUPS - 1)
            for u in range(HALVES):
                norm_scale((BATCH - 1) * HALVES + u)

        @block.scalar
        def _(act):
            def aux(b, g, n, kind, t, bank):
                if kind == "t":
                    half, k = t // KT, t % KT
                    act.wait_ge(x_turned, (b + 1) * 2 * KT + t + 1)
                    nc.scalar.copy(x_hi[:, k, half * CHUNK:(half + 1) * CHUNK], aux_ps[:, bank]).then_inc(x_hi_made, 1)
                elif kind == "q":
                    which, half = t // 2, t % 2
                    m = n + 2
                    act.wait_ge(qk_ready, 4 * m + t + 1)
                    need(act, qk_split, 4 * m + t - 1)
                    lift = QUERY_LIFT / WEIGHT_LIFT if which == 0 else 1.0 / WEIGHT_LIFT
                    group = (g + 2) % GROUPS
                    nc.scalar.activation(qk_full[:, t % 2], aux_ps[:, bank], ACT.Identity, scale=lift,
                                         bias=bias_cols[:, which, group:group + 1]).then_inc(qk_full_made, 1)
                    act.wait_ge(qk_full_made, 4 * m + t + 1)
                    if not (isinstance(m, int) and m == 0):
                        act.wait_ge(stacked[(g + 1) % 2], stacked_count(m - 1, b, g))
                    nc.scalar.copy(qk_hi[:, which, half * CHUNK:(half + 1) * CHUNK],
                                   qk_full[:, t % 2]).then_inc(qk_hi_made, 1)

            def stacked_count(m, b, g):
                return (b * 2 + (g + 1) // 2 + 1) * STACK_DMAS * 16

            def exp(n, unit):
                e = n * UNITS + unit
                tiles = n * HALVES * KEY_TILES + unit // 2
                act.wait_ge(scored, e + 1)
                need(act, weighed, tiles - 1)
                kt = (unit % HALF_UNITS) // 2
                if 2 <= kt < POOLED + 2:
                    half = n * HALVES + unit // HALF_UNITS
                    done = half * 2 * (POOLED - 1) + 2 * max(kt - 3, 0) + unit % 2 + 1
                    act.wait_ge(pooled, done)
                nc.scalar.activation(probs[:, unit % PROBS], score_ps[:, unit % 2], ACT.Exp,
                                     scale=exp_scale[:, 0:1]).then_inc(exp_made, 1)

            def keep_mix(n, half):
                h = n * HALVES + half
                act.wait_ge(weighed, (h + 1) * KEY_TILES)
                need(act, z_made, h - 1)
                nc.scalar.copy(mixed[:, half], mix_ps[:]).then_inc(mix_kept, 1)

            def z_high(n, half, g):
                h = n * HALVES + half
                act.wait_ge(z_made, h + 1)
                nc.scalar.copy(z_hi[:, g, half * CHUNK:(half + 1) * CHUNK], z[:, half]).then_inc(z_hi_made, 1)

            def max_rows_out(n, bank):
                act.wait_ge(rows_turned, n + 1)
                need(act, rows_stacked, 16 * n)
                nc.scalar.mul(max_rows[:, :], aux_ps[0:MAXES // HALVES, bank, 0:P], 1.0 / MAX_LIFT
                              ).then_inc(rows_made, 1)

            for t in range(2 * KT):
                aux(-1, 0, 0, "t", t, (t + 1) % 2)
            for n in range(2):
                for t in range(4):
                    aux(0, n - 2, n - 2, "q", t, (t + 1) % 2)
            max_rows_out(0, 1)

            def body(b):
                for g in range(GROUPS):
                    n = b * GROUPS + g
                    work = unit_work(b, g)
                    position = 0
                    for unit in range(UNITS):
                        exp(n, unit)
                        if unit == HALF_UNITS + 1:
                            keep_mix(n, 0)
                        if unit == 4 and not (is_first(b) and g == 0):
                            z_high(n - 1, 1, (g - 1) % GROUPS)
                        if unit == HALF_UNITS + 5:
                            if g == 0 and not is_first(b):
                                act.wait_ge(o_ready, b * TILES)
                            z_high(n, 0, g)
                        for kind, t in work[unit]:
                            aux(b, g, n, kind, t, (g + position) % 2)
                            position += 1
                    if not (is_last(b) and g == GROUPS - 1):
                        max_rows_out(n + 1, (g + position) % 2)
                    keep_mix(n, 1)

            over_batches(act, body)
            z_high(STEPS - 1, 1, GROUPS - 1)

        @block.vector
        def _(dve):
            def aux(b, g, n, kind, t, bank):
                if kind == "t":
                    half, k = t // KT, t % KT
                    at = slice(half * CHUNK, (half + 1) * CHUNK)
                    dve.wait_ge(x_hi_made, (b + 1) * 2 * KT + t + 1)
                    nc.vector.tensor_tensor(x_lo[:, k, at], aux_ps[:, bank], x_hi[:, k, at],
                                            ALU.subtract).then_inc(x_split, 1)
                elif kind == "v":
                    dve.wait_ge(v_ready, b * TILES + t + 1)
                    nc.vector.scalar_tensor_tensor(out=v[:, t], in0=aux_ps[:, bank], scalar=1.0 / WEIGHT_LIFT,
                                                   in1=bias_rows[:, 0], op0=ALU.mult, op1=ALU.add
                                                   ).then_inc(v_made, 1)
                elif kind == "o":
                    u, tt = t // TT, t % TT
                    row = (b - 1) * TILES + t
                    if tt == 0:
                        dve.wait_ge(skip_loaded[u], 16 * b)
                        dve.wait_ge(stored[u], 16 * b)
                    dve.wait_ge(o_ready, row + 1)
                    nc.vector.scalar_tensor_tensor(out=total[:, u, tt], in0=aux_ps[:, bank], scalar=out_scale[:, 0:1],
                                                   in1=x_tok[:, u, tt], op0=ALU.mult, op1=ALU.add
                                                   ).then_inc(skipped, 1)
                elif kind == "m":
                    tile = (n + 1) * MAXES + t
                    dve.wait_ge(m_ready, tile + 1)
                    if t == 0:
                        need(dve, row_max_made, n + 1)
                    nc.vector.tensor_reduce(maxes[:, t // HALVES, t % HALVES:t % HALVES + 1], aux_ps[:, bank],
                                            AX.X, ALU.max).then_inc(maxed, 1)

            def combine(n):
                dve.wait_ge(maxed, (n + 1) * MAXES)
                need(dve, rows_turned, n)
                nc.vector.tensor_reduce(row_max[:], maxes[:], AX.X, ALU.max, negate=True).then_inc(row_max_made, 1)

            def invert(n, half):
                h = n * HALVES + half
                dve.wait_ge(weighed, (h + 1) * KEY_TILES)
                need(dve, z_made, h - 1)
                nc.vector.reciprocal(recip[:, half], sum_ps[:]).then_inc(recip_made, 1)

            def make_z(n, half):
                h = n * HALVES + half
                dve.wait_ge(recip_made, h + 1)
                dve.wait_ge(mix_kept, h + 1)
                need(dve, z_split, h - 1)
                nc.vector.scalar_tensor_tensor(out=z[:, half], in0=mixed[:, half], scalar=QUERY_LIFT,
                                               in1=recip[:, half], op0=ALU.mult, op1=ALU.mult).then_inc(z_made, 1)

            def add_bias(b, u):
                for tt in range(TT):
                    dve.wait_ge(skipped, b * TILES + u * TT + tt + 1)
                    nc.vector.tensor_tensor(total[:, u, tt], total[:, u, tt], bias_rows[:, 1],
                                            ALU.add).then_inc(residual, 1)

            def take_moments(b, u):
                rows = b * TILES + u * TT
                if u > 0:
                    dve.wait_ge(moments_made, rows)
                for tt in range(TT):
                    dve.wait_ge(residual, rows + tt + 1)
                    nc.vector.bn_stats(stats[:, tt], total[:, u, tt]).then_inc(stats_made, 1)
                if u > 0:
                    dve.wait_ge(normed, rows)
                dve.wait_ge(stats_made, rows + TT)
                dve.sem_inc(stats_seen, 1)
                for tt in range(TT):
                    nc.vector.bn_aggr(moments[:, tt], stats[:, tt]).then_inc(moments_made, 1)

            def normalise(b, u):
                dve.wait_ge(rstd_made, b * HALVES + u + 1)
                for tt in range(TT):
                    nc.vector.tensor_scalar(total[:, u, tt], total[:, u, tt], moments[:, tt, 0:1], rstd[:, tt:tt + 1],
                                            ALU.subtract, ALU.mult).then_inc(normed, 1)

            nc.vector.memset(keys[3 * HEAD:ROWS, :, :, :], MAX_LIFT).then_inc(key_ones_set, 1)
            for t in range(2 * KT):
                aux(-1, 0, 0, "t", t, (t + 1) % 2)
            for t in range(MAXES):
                aux(0, 0, -1, "m", t, (t + 1) % 2)
            combine(0)

            def body(b):
                for g in range(GROUPS):
                    n = b * GROUPS + g
                    work = unit_work(b, g)
                    position = 0
                    for unit in range(UNITS):
                        if unit == 1 and not (is_first(b) and g == 0):
                            invert(n - 1, 1)
                            make_z(n - 1, 1)
                        if unit == HALF_UNITS + 2:
                            invert(n, 0)
                            make_z(n, 0)
                        for kind, t in work[unit]:
                            aux(b, g, n, kind, t, (g + position) % 2)
                            position += 1
                        if g == 0 and not is_first(b):
                            if unit == 7:
                                add_bias(b - 1, 0)
                                take_moments(b - 1, 0)
                            if unit == NORM_UNITS[0] + 1:
                                normalise(b - 1, 0)
                                add_bias(b - 1, 1)
                                take_moments(b - 1, 1)
                            if unit == NORM_UNITS[1] + 1:
                                normalise(b - 1, 1)
                    if not (is_last(b) and g == GROUPS - 1):
                        combine(n + 1)

            over_batches(dve, body)
            invert(STEPS - 1, 1)
            make_z(STEPS - 1, 1)
            for t in range(TILES):
                aux(BATCH, 0, 0, "o", t, (t + 1) % 2)
            for u in range(HALVES):
                add_bias(BATCH - 1, u)
                take_moments(BATCH - 1, u)
                normalise(BATCH - 1, u)

        @block.tensor
        def _(pe):
            PRODUCTS = ((0, 0), (0, 1), (1, 0))
            w_parts, x_parts, z_parts = (w_hi, w_lo), (x_hi, x_lo), (z_hi, z_lo)

            def wait_taken(b, g, n, kind, t):
                if kind == "t":
                    pe.wait_ge(x_split, (b + 1) * 2 * KT + t + 1)
                elif kind == "v":
                    pe.wait_ge(v_made, b * TILES + t + 1)
                elif kind == "o":
                    pe.wait_ge(skipped, (b - 1) * TILES + t + 1)
                elif kind == "q":
                    pe.wait_ge(qk_full_made, 4 * (n + 2) + t + 1)
                elif kind == "m":
                    pe.wait_ge(maxed, (n + 1) * MAXES + t + 1)
                elif kind == "r":
                    pe.wait_ge(rows_made, n + 2)

            def tile(b, g, n, kind, t, bank):
                if kind == "t":
                    half, k = t // KT, t % KT
                    pe.wait_ge(rows_loaded[half], 16 * (b + 2))
                    for tt in range(TT):
                        last = nc.tensor.transpose(aux_ps[:, bank, tt * P:(tt + 1) * P],
                                                   x_tok[:, half, tt, k * P:(k + 1) * P], ident)
                    last.then_inc(x_turned, 1)
                elif kind == "q":
                    which, half = t // 2, t % 2
                    group = (g + 2) % GROUPS
                    pe.wait_ge(x_split, (b + 1 if g < 2 else b + 2) * 2 * KT)
                    for k in range(KT):
                        for i, (a, c) in enumerate(PRODUCTS):
                            last = nc.tensor.matmul(aux_ps[:, bank], w_parts[a][:, which, k, group * P:(group + 1) * P],
                                                    x_parts[c][:, k, half * CHUNK:(half + 1) * CHUNK],
                                                    start=(k == 0 and i == 0), stop=(k == KT - 1 and i == 2))
                    last.then_inc(qk_ready, 1)
                elif kind in ("v", "o"):
                    if kind == "v":
                        parts, which, done = x_parts, WV, v_ready
                        pe.wait_ge(x_split, (b + 1) * 2 * KT)
                    else:
                        parts, which, done = z_parts, WO, o_ready
                        pe.wait_ge(z_split, b * GROUPS * HALVES)
                    for k in range(KT):
                        for i, (a, c) in enumerate(PRODUCTS):
                            last = nc.tensor.matmul(aux_ps[:, bank], parts[c][:, k, t * P:(t + 1) * P],
                                                    w_parts[a][:, which, k], start=(k == 0 and i == 0),
                                                    stop=(k == KT - 1 and i == 2))
                    last.then_inc(done, 1)
                elif kind == "m":
                    j, qt, kh = t // (KEY_TILES * HALVES), t // HALVES % KEY_TILES, t % HALVES
                    buffer = (g + 1) % 2
                    if t == 0:
                        pe.wait_ge(stacked[buffer], (b * 2 + (g + 1) // 2 + 1) * STACK_DMAS * 16)
                    last = nc.tensor.matmul(aux_ps[:, bank], queries[0:3 * HEAD, buffer, j, qt * P:(qt + 1) * P],
                                            keys[0:3 * HEAD, buffer, j, kh * CHUNK:(kh + 1) * CHUNK],
                                            start=True, stop=True)
                    last.then_inc(m_ready, 1)
                elif kind == "r":
                    pe.wait_ge(row_max_made, n + 2)
                    nc.tensor.transpose(aux_ps[0:MAXES // HALVES, bank, 0:P], row_max[:], ident).then_inc(rows_turned, 1)

            history = []

            def aux(b, g, n, kind, t, bank):
                if len(history) == 2:
                    wait_taken(*history.pop(0))
                history.append((b, g, n, kind, t))
                tile(b, g, n, kind, t, bank)

            def scores(n, g, unit):
                half, kt, pair = unit // HALF_UNITS, (unit % HALF_UNITS) // 2, unit % 2
                buffer = g % 2
                if unit == 0:
                    pe.wait_ge(rows_stacked, 16 * (n + 1))
                need(pe, exp_made, n * UNITS + unit - 1)
                for i in range(PAIR):
                    j = PAIR * pair + i
                    last = nc.tensor.matmul(score_ps[:, unit % 2, i], keys[:, buffer, j, kt * P:(kt + 1) * P],
                                            queries[:, buffer, j, half * CHUNK:(half + 1) * CHUNK],
                                            start=True, stop=True)
                last.then_inc(scored, 1)

            def weigh(b, n, g, half, kt):
                h = n * HALVES + half
                pe.wait_ge(exp_made, n * UNITS + half * HALF_UNITS + 2 * kt + 2)
                if g == 0 and half == 0 and kt == 0:
                    pe.wait_ge(v_made, (b + 1) * TILES)
                if kt == 0:
                    need(pe, mix_kept, h)
                for j in range(G_HEADS):
                    slot = (2 * kt + j // PAIR) % PROBS
                    last = nc.tensor.matmul(mix_ps[j * HEAD:(j + 1) * HEAD, :],
                                            v[:, kt, (G_HEADS * g + j) * HEAD:(G_HEADS * g + j + 1) * HEAD],
                                            probs[:, slot, j % PAIR], start=(kt == 0), stop=(kt == KEY_TILES - 1))
                if kt == POOLED:
                    pe.wait_ge(pooled, (h + 1) * 2 * (POOLED - 1))
                    need(pe, recip_made, h)
                    for j in range(G_HEADS):
                        nc.tensor.matmul(sum_ps[j * HEAD:(j + 1) * HEAD, :], ones[:, 0:HEAD], prob_sums[:, j],
                                         start=True, stop=False)
                if kt >= POOLED:
                    for j in range(G_HEADS):
                        slot = (2 * kt + j // PAIR) % PROBS
                        last = nc.tensor.matmul(sum_ps[j * HEAD:(j + 1) * HEAD, :], ones[:, 0:HEAD],
                                                probs[:, slot, j % PAIR], start=False, stop=(kt == KEY_TILES - 1))
                last.then_inc(weighed, 1)

            pe.wait_ge(key_ones_set, 1)
            for t in range(2 * KT):
                aux(-1, 0, -4, "t", t, (t + 1) % 2)
            for n in range(2):
                for t in range(4):
                    aux(-1, n + 2, n - 2, "q", t, (t + 1) % 2)
            for t in range(MAXES):
                aux(0, -1, -1, "m", t, (t + 1) % 2)
            aux(0, -1, -1, "r", 0, 1)

            def body(b):
                before = b * GROUPS - 1
                history[:] = [(b - 1, GROUPS - 1, before, "m", MAXES - 1), (b - 1, GROUPS - 1, before, "r", 0)]
                for g in range(GROUPS):
                    n = b * GROUPS + g
                    work = unit_work(b, g)
                    position = 0
                    for unit in range(UNITS):
                        scores(n, g, unit)
                        for kind, t in work[unit]:
                            aux(b, g, n, kind, t, (g + position) % 2)
                            position += 1
                        if unit >= 3 and unit % 2 == 1:
                            before = unit // 2 - 1
                            weigh(b, n, g, before // KEY_TILES, before % KEY_TILES)
                    if not (is_last(b) and g == GROUPS - 1):
                        aux(b, g, n, "r", 0, (g + position) % 2)
                    weigh(b, n, g, 1, KEY_TILES - 1)

            over_batches(pe, body)
            for t in range(TILES):
                aux(BATCH, 0, STEPS, "o", t, (t + 1) % 2)


def build(nc, args, out):
    between = [nc.dram_tensor("after_stage%d" % n, (TOKENS, D), F32, kind="Internal").ap() for n in range(3)]
    with ExitStack() as stack:
        ident = stack.enter_context(nc.sbuf_tensor("ident", [P, P], F32))
        ones = stack.enter_context(nc.sbuf_tensor("ones", [P, P], F32))
        setup_constants(nc, ident, ones)
        retention_stage(nc, args, ident, between[0])
        quantized_ffn_stage(nc, args, ident, between[0], between[1])
        attention_stage(nc, args, ident, ones, between[1], between[2])
        ternary_ffn_stage(nc, args, ident, ones, between[2], out)


def retention_stage(nc, args, ident, x_out):
    with ExitStack() as stack:
        w_hi = stack.enter_context(nc.sbuf_tensor("ret_w_hi", [P, 4, KT, D], F32R))
        w_lo = stack.enter_context(nc.sbuf_tensor("ret_w_lo", [P, 4, KT, D], F32R))
        split_weights(nc, "ret_w_", [args["L0_attn_" + n] for n in ("Wq", "Wv", "Wg", "Wo")], w_hi, w_lo)
        retention_phase(nc, args["L0_attn_x"], args["L0_attn_x_T"], x_out, ident[:], w_hi, w_lo,
                        args["L0_attn_beta"], args["L0_attn_ln_w"], args["L0_attn_ln_b"])


def quantized_ffn_stage(nc, args, ident, x_in, x_out):
    hidden_tiles = args["L0_ffn_gate_w"].shape[1] // P
    with ExitStack() as stack:
        gate_scale = stack.enter_context(nc.sbuf_tensor("gate_scale", [P, hidden_tiles], F32))
        up_scale = stack.enter_context(nc.sbuf_tensor("up_scale", [P, hidden_tiles], F32))
        down_scale = stack.enter_context(nc.sbuf_tensor("down_scale", [P, D], F32))
        w_gate = stack.enter_context(nc.sbuf_tensor("w_gate", [P, KT, hidden_tiles * P], F16))
        w_up = stack.enter_context(nc.sbuf_tensor("w_up", [P, KT, hidden_tiles * P], F16))
        w_down = stack.enter_context(nc.sbuf_tensor("w_down", [P, hidden_tiles, D], F32R))
        load_scales(nc, "ffn0", [(args["L0_ffn_gate_scale"], gate_scale), (args["L0_ffn_up_scale"], up_scale)],
                    [(args["L0_ffn_down_scale"], down_scale)])
        fp8_weights(nc, (args["L0_ffn_gate_w"], args["L0_ffn_up_w"], args["L0_ffn_down_w"]), (w_gate, w_up, w_down))
        ffn_phase(nc, "ffn0_", x_in, x_out, ident[:], w_gate, w_up, w_down, hidden_tiles, ACT.Silu,
                  gate_scale[:], up_scale[:], down_scale[:], F32R)


def attention_stage(nc, args, ident, ones, x_in, x_out):
    with ExitStack() as stack:
        w_hi = stack.enter_context(nc.sbuf_tensor("att_w_hi", [P, 4, KT, D], F16))
        w_lo = stack.enter_context(nc.sbuf_tensor("att_w_lo", [P, 4, KT, D], F16))
        bias_cols = stack.enter_context(nc.sbuf_tensor("att_bias_cols", [P, 2, KT], F32))
        bias_rows = stack.enter_context(nc.sbuf_tensor("att_bias_rows", [P, 2, D], F32))
        exp_scale = stack.enter_context(nc.sbuf_tensor("att_exp_scale", [P, 1], F32))
        out_scale = stack.enter_context(nc.sbuf_tensor("att_out_scale", [P, 1], F32))
        names = ("q", "k", "v", "o")
        lora_weights(nc, [args["L1_attn_W" + n] for n in names], [args["L1_attn_A" + n] for n in names],
                     [args["L1_attn_B" + n] for n in names], [args["L1_attn_b" + n] for n in names],
                     w_hi, w_lo, bias_cols, bias_rows, exp_scale, out_scale)
        attention_phase(nc, x_in, x_out, ident[:], ones, w_hi, w_lo, bias_cols, bias_rows, exp_scale, out_scale)


def ternary_ffn_stage(nc, args, ident, ones, x_in, x_out):
    hidden_tiles = args["L1_ffn_w1"].shape[1] // P
    with ExitStack() as stack:
        w1 = stack.enter_context(nc.sbuf_tensor("w1", [P, KT, hidden_tiles * P], F16))
        w2 = stack.enter_context(nc.sbuf_tensor("w2", [P, KT, hidden_tiles * P], F16))
        w3 = stack.enter_context(nc.sbuf_tensor("w3", [P, hidden_tiles, D], F16))
        ternary_weights(nc, ones, (args["L1_ffn_w1"], args["L1_ffn_w2"], args["L1_ffn_w3"]), (w1, w2, w3))
        ffn_phase(nc, "ffn1_", x_in, x_out, ident[:], w1, w2, w3, hidden_tiles, ACT.Sigmoid, None, None, None, F16)


_TRANSPOSED = ('L0_attn_Wq', 'L0_attn_Wv', 'L0_attn_Wg', 'L0_attn_Wo', 'L1_attn_Wq', 'L1_attn_Wk', 'L1_attn_Wv',
               'L1_attn_Wo', 'L1_attn_Aq', 'L1_attn_Ak', 'L1_attn_Av', 'L1_attn_Ao', 'L1_ffn_w1', 'L1_ffn_w2',
               'L1_ffn_w3')


def kernel(**inputs):
    import numpy as _np
    import concourse.bacc as _bacc
    from concourse import mybir as _mybir
    from concourse.bass_utils import run_bass_kernel_spmd as _run

    nc = _bacc.Bacc("TRN2", target_bir_lowering=False, num_devices=1)
    arrays, args = {}, {}

    def give(name, array):
        a = _np.ascontiguousarray(array)
        arrays[f"in_{name}"] = a
        args[name] = nc.dram_tensor(f"in_{name}", a.shape, _mybir.dt.from_np(a.dtype), kind="ExternalInput").ap()

    for name, value in inputs.items():
        a = _np.asarray(value)
        if name == 'L0_attn_x':
            rows = a.reshape(-1, a.shape[-1])
            give(name, rows)
            give(name + "_T", rows.T)
        else:
            give(name, a.T if name in _TRANSPOSED else a)
    shape = _np.asarray(inputs['L0_attn_x']).shape
    out = nc.dram_tensor("out", (shape[0] * shape[1], shape[2]), _mybir.dt.float32, kind="ExternalOutput").ap()
    build(nc, args, out)
    r = _run(nc, [arrays], core_ids=[0])
    return r.results[0]["out"].reshape(shape)
```

```python
from contextlib import ExitStack

import numpy as np
import concourse.bass as bass
from concourse import mybir

F32 = mybir.dt.float32
F32R = mybir.dt.float32r
F16 = mybir.dt.float16
U32 = mybir.dt.uint32
ALU = mybir.AluOpType
ACT = mybir.ActivationFunctionType
AX = mybir.AxisListType

P = 128
D = 512
KT = D // P
BATCH, SEQ = 4, 1024
TOKENS = BATCH * SEQ
CHUNK = 512
CHUNKS = TOKENS // CHUNK
TT = CHUNK // P
PAIRS = CHUNKS // 2
LN_EPS = 1e-5


def need(eng, sem, value):
    if isinstance(value, int) and value <= 0:
        return
    eng.wait_ge(sem, value)


def over_pairs(eng, body):
    body(0, True, False)
    with eng.Fori(1, PAIRS - 1) as i:
        body(i, False, False)
    body(PAIRS - 1, False, True)


def tokens_of(dram, c):
    return dram[bass.ds(c * CHUNK, CHUNK), :].rearrange("(t p) d -> p t d", p=P)


def stage_semaphores(nc, stack, tag):
    taken = []

    def give_back():
        nc.clear_and_free_semaphores(taken)
        nc.all_engine_barrier()

    def sem(name):
        taken.append(nc.alloc_semaphore(name=tag + name))
        return taken[-1]

    stack.callback(give_back)
    return sem


def setup_constants(nc, ident, ones):
    with ExitStack() as stack:
        ident_cleared = stack.enter_context(nc.semaphore("ident_cleared"))
        constants_made = stack.enter_context(nc.semaphore("constants_made"))
        block = stack.enter_context(nc.Block())
        @block.gpsimd
        def _(pool):
            nc.gpsimd.memset(ident[:], 0.0).then_inc(ident_cleared, 1)
            nc.gpsimd.memset(ones[:], 1.0).then_inc(constants_made, 1)
            pool.wait_ge(ident_cleared, 1)
            nc.gpsimd.affine_select(out=ident[:], in_=ident[:], compare_op=ALU.not_equal, fill=1.0, base=0,
                                    pattern=[[-1, P]], channel_multiplier=1).then_inc(constants_made, 1)
            pool.wait_ge(constants_made, 2)


def fp8_weights(nc, sources, targets, columns, rows):
    PIECE = 2048
    RING = 3
    OVERFLOW = 1.1 * 2.0 ** 119
    pieces = []
    for source, target in zip(sources, targets):
        tiles = PIECE // target.shape[2] or 1
        for first in range(0, target.shape[1], tiles):
            pieces.append((source, target, first, min(first + tiles, target.shape[1])))
    N = len(pieces)
    with ExitStack() as stack:
        raw = stack.enter_context(nc.sbuf_tensor("fp8_raw", [P, RING, PIECE], F32))
        addend = stack.enter_context(nc.sbuf_tensor("fp8_addend", [P, RING, PIECE], F32))
        shifted = stack.enter_context(nc.sbuf_tensor("fp8_shifted", [P, RING, PIECE], F32))
        overflow = stack.enter_context(nc.sbuf_tensor("fp8_overflow", [P, RING, PIECE], F32))
        loaded = [stack.enter_context(nc.semaphore("fp8_loaded%d" % r)) for r in range(RING)]
        exponent_made = stack.enter_context(nc.semaphore("fp8_exponent_made"))
        addend_made = stack.enter_context(nc.semaphore("fp8_addend_made"))
        shifted_made = stack.enter_context(nc.semaphore("fp8_shifted_made"))
        rounded = stack.enter_context(nc.semaphore("fp8_rounded"))
        overflow_made = stack.enter_context(nc.semaphore("fp8_overflow_made"))
        vectors_loaded = stack.enter_context(nc.semaphore("fp8_vectors_loaded"))
        done = stack.enter_context(nc.semaphore("fp8_done"))
        block = stack.enter_context(nc.Block())

        def view(buffer, n):
            _, target, first, last = pieces[n]
            return buffer[:, n % RING, 0:(last - first) * target.shape[2]]

        @block.sync
        def _(sp):
            for n, (source, target, first, last) in enumerate(pieces):
                need(sp, shifted_made, n - RING + 1)
                sp.dma_start(view(raw, n).rearrange("p (t h) -> p t h", t=last - first),
                             source.rearrange("(t p) h -> p t h", p=P)[:, first:last]).then_inc(loaded[n % RING], 16)
            for source, target in columns:
                with nc.allow_non_contiguous_dma(reason="a short vector, one channel for each partition"):
                    sp.dma_start(target[:], source.rearrange("(t p) -> p t", p=P)).then_inc(vectors_loaded, 16)
            for source, target in rows:
                sp.dma_start(target[:], source.rearrange("(o n) -> o n", o=1).partition_broadcast(P)
                             ).then_inc(vectors_loaded, 16)
            sp.wait_ge(vectors_loaded, 16 * (len(columns) + len(rows)))

        @block.gpsimd
        def _(pool):
            for n in range(N):
                pool.wait_ge(addend_made, n + 1)
                need(pool, done, n - RING + 1)
                nc.gpsimd.tensor_tensor(view(shifted, n), view(addend, n), view(raw, n),
                                        ALU.subtract).then_inc(shifted_made, 1)

        @block.scalar
        def _(act):
            for n in range(N):
                act.wait_ge(rounded, n + 1)
                need(act, done, n - RING + 1)
                nc.scalar.mul(view(overflow, n), view(shifted, n), OVERFLOW).then_inc(overflow_made, 1)

        @block.vector
        def _(dve):
            def make_addend(n):
                dve.wait_ge(loaded[n % RING], 16 * (n // RING + 1))
                need(dve, rounded, n - RING + 1)
                nc.vector.tensor_scalar(view(addend, n).bitcast(U32), view(raw, n).bitcast(U32), 0x7F800000, None,
                                        ALU.bitwise_and).then_inc(exponent_made, 1)
                dve.wait_ge(exponent_made, n + 1)
                nc.vector.tensor_scalar(view(addend, n), view(addend, n), 1.5 * 2.0 ** 20, 1.5 * 2.0 ** 14,
                                        ALU.mult, ALU.max).then_inc(addend_made, 1)

            def shift_back(n):
                dve.wait_ge(shifted_made, n + 1)
                nc.vector.tensor_tensor(view(shifted, n), view(addend, n), view(shifted, n),
                                        ALU.subtract).then_inc(rounded, 1)

            def finish(n):
                _, target, first, last = pieces[n]
                dve.wait_ge(overflow_made, n + 1)
                nc.vector.scalar_tensor_tensor(out=target[:, first:last].rearrange("p t h -> p (t h)"),
                                               in0=view(overflow, n), scalar=0.0, in1=view(shifted, n),
                                               op0=ALU.mult, op1=ALU.add).then_inc(done, 1)

            for n in range(N + 2):
                if n < N:
                    make_addend(n)
                if 1 <= n <= N:
                    shift_back(n - 1)
                if n >= 2:
                    finish(n - 2)
            dve.wait_ge(done, N)


class TernaryWeights:

    RING = 3

    def __init__(self, nc, stack, sources, targets, sums_scratch):
        def sbuf(name, shape, dtype=F32):
            return stack.enter_context(nc.sbuf_tensor("ternary_" + name, shape, dtype))

        def sem(name):
            return stack.enter_context(nc.semaphore("ternary_" + name))

        self.nc, self.sources, self.targets, self.sums_scratch = nc, sources, targets, sums_scratch
        self.tiles = [source.shape[0] // P for source in sources]
        width = sources[0].shape[0] * sources[0].shape[1] // P
        self.count = P * width
        self.pieces = []
        for m in range(len(sources)):
            step = -(-self.tiles[m] // 4) * sources[m].shape[1]
            self.pieces += [(m, at, min(at + step, width)) for at in range(0, width, step)]
        widest = max(end - at for _, at, end in self.pieces)
        self.raw = sbuf("raw", [P, len(sources), width])
        self.below = sbuf("below", [P, widest], F16)
        self.result = sbuf("result", [P, self.RING, widest], F16)
        self.piece_sums = sbuf("piece_sums", [P, len(self.pieces)])
        self.sums = sbuf("sums", [P, len(sources)])
        self.all_sums = sbuf("all_sums", [P, P, len(sources)])
        self.total = sbuf("total", [P, len(sources)])
        self.gamma_half = sbuf("gamma_half", [P, len(sources)])
        self.minus_half = sbuf("minus_gamma_half", [P, len(sources)])
        self.loaded = [sem("loaded%d" % m) for m in range(len(sources))]
        self.summed, self.sums_made = sem("summed"), sem("sums_made")
        self.sums_out, self.sums_back, self.gamma_made = sem("sums_out"), sem("sums_back"), sem("gamma_made")
        self.below_made, self.made = sem("below_made"), sem("made")
        self.stored = [sem("stored%d" % r) for r in range(self.RING)]

    def load(self, eng):
        for m, source in enumerate(self.sources):
            eng.dma_start(self.raw[:, m].rearrange("p (t h) -> p t h", t=self.tiles[m]),
                          source.rearrange("(t p) h -> p t h", p=P)).then_inc(self.loaded[m], 16)

    def sum_piece(self, dve, n):
        m, at, end = self.pieces[n]
        dve.wait_ge(self.loaded[m], 16)
        self.nc.vector.tensor_reduce(self.piece_sums[:, n:n + 1], self.raw[:, m, at:end], AX.X, ALU.add,
                                     apply_absolute_value=True).then_inc(self.summed, 1)

    def sum_matrices(self, dve):
        dve.wait_ge(self.summed, len(self.pieces))
        self.nc.vector.tensor_reduce(self.sums[:], self.piece_sums[:].rearrange("p (m n) -> p m n", n=4), AX.X,
                                     ALU.add).then_inc(self.sums_made, 1)

    def gather_sums(self, act):
        act.wait_ge(self.sums_made, 1)
        act.dma_start(self.sums_scratch, self.sums[:]).then_inc(self.sums_out, 16)
        act.wait_ge(self.sums_out, 16)
        act.dma_start(self.all_sums[:].rearrange("p q m -> p (q m)"),
                      self.sums_scratch.rearrange("(o q) m -> o (q m)", o=1).partition_broadcast(P)
                      ).then_inc(self.sums_back, 16)

    def make_gamma(self, dve):
        dve.wait_ge(self.sums_back, 16)
        self.nc.vector.tensor_reduce(self.total[:], self.all_sums[:].rearrange("p q m -> p m q"), AX.X,
                                     ALU.add).then_inc(self.gamma_made, 1)
        dve.wait_ge(self.gamma_made, 1)
        self.nc.vector.tensor_scalar(self.total[:], self.total[:], 1.0 / self.count, 1e-8,
                                     ALU.mult, ALU.add).then_inc(self.gamma_made, 1)
        dve.wait_ge(self.gamma_made, 2)
        self.nc.vector.tensor_scalar(self.gamma_half[:], self.total[:], 0.5, None,
                                     ALU.mult).then_inc(self.gamma_made, 1)
        self.nc.vector.tensor_scalar(self.minus_half[:], self.total[:], -0.5, None,
                                     ALU.mult).then_inc(self.gamma_made, 1)

    def quantise(self, dve, n):
        m, at, end = self.pieces[n]
        dve.wait_ge(self.gamma_made, 4)
        need(dve, self.made, n)
        self.nc.vector.tensor_scalar(self.below[:, 0:end - at], self.raw[:, m, at:end], self.minus_half[:, m:m + 1],
                                     None, ALU.is_lt).then_inc(self.below_made, 1)
        dve.wait_ge(self.below_made, n + 1)
        need(dve, self.stored[n % self.RING], 16 * (n // self.RING))
        self.nc.vector.scalar_tensor_tensor(out=self.result[:, n % self.RING, 0:end - at], in0=self.raw[:, m, at:end],
                                            scalar=self.gamma_half[:, m:m + 1], in1=self.below[:, 0:end - at],
                                            op0=ALU.is_gt, op1=ALU.subtract).then_inc(self.made, 1)

    def store(self, act, n):
        m, at, end = self.pieces[n]
        act.wait_ge(self.made, n + 1)
        act.dma_start(self.targets[m][:, at:end], self.result[:, n % self.RING, 0:end - at]
                      ).then_inc(self.stored[n % self.RING], 16)

    def finish(self, act):
        for r in range(self.RING):
            act.wait_ge(self.stored[r], 16 * len(range(r, len(self.pieces), self.RING)))


def retention_phase(nc, x_rows, x_turned, x_out, ident, weights, beta, ln_w, ln_b):
    tag = "ret_"
    WV, WQ, WG, WO = range(4)
    with ExitStack() as stack:
        def sbuf(name, shape, dtype=F32):
            return stack.enter_context(nc.sbuf_tensor(tag + name, shape, dtype))

        sem = stage_semaphores(nc, stack, tag)

        w_raw = sbuf("w_raw", [P, 2, KT, D])
        w_hi = sbuf("w_hi", [P, 4, KT, D], F32R)
        w_lo = sbuf("w_lo", [P, 4, KT, D], F32R)
        x_t = sbuf("x_t", [P, KT, CHUNK])
        x_hi = sbuf("x_hi", [P, KT, CHUNK], F32R)
        x_lo = sbuf("x_lo", [P, KT, CHUNK], F32R)
        x_tok = sbuf("x_tok", [P, 2, TT, D])
        state = sbuf("state", [P, 2, KT, CHUNK])
        q_kept = sbuf("q_kept", [P, TT, D])
        y = sbuf("y", [P, TT, D])
        gate = sbuf("gate", [P, KT, CHUNK])
        z = sbuf("z", [P, KT, CHUNK])
        z_hi = sbuf("z_hi", [P, KT, CHUNK], F32R)
        z_lo = sbuf("z_lo", [P, KT, CHUNK], F32R)
        total = sbuf("total", [P, 2, TT, D])
        decay_in = sbuf("decay_in", [P, KT])
        decay = sbuf("decay", [P, KT])
        ln_w_col = sbuf("ln_w_col", [P, KT])
        ln_b_col = sbuf("ln_b_col", [P, KT])
        minus_half = sbuf("minus_half", [P, TT])
        eps = sbuf("eps", [P, TT])
        y_stats = sbuf("y_stats", [P, TT, 6])
        y_moments = sbuf("y_moments", [P, TT, 2])
        y_var_eps = sbuf("y_var_eps", [P, TT])
        y_rstd = sbuf("y_rstd", [P, TT])
        stats = sbuf("stats", [P, TT, 6])
        moments = sbuf("moments", [P, TT, 2])
        var_eps = sbuf("var_eps", [P, TT])
        rstd = sbuf("rstd", [P, TT])
        chan_ps = stack.enter_context(nc.psum_tensor(tag + "chan_ps", [P, KT, CHUNK], F32))
        tok_ps = stack.enter_context(nc.psum_tensor(tag + "tok_ps", [P, TT, D], F32))

        w_loaded = (sem("w_loaded0"), sem("w_loaded1"))
        w_hi_made, w_split = sem("w_hi_made"), sem("w_split")
        vectors_loaded, decay_made, constants_set = sem("vectors_loaded"), sem("decay_made"), sem("constants_set")
        x_t_loaded, x_hi_made, x_split = sem("x_t_loaded"), sem("x_hi_made"), sem("x_split")
        x_loaded = (sem("x_loaded0"), sem("x_loaded1"))
        stored = (sem("stored0"), sem("stored1"))
        v_ready, scanned = sem("v_ready"), sem("scanned")
        q_ready, q_out = sem("q_ready"), sem("q_out")
        state_turned, y_made = sem("state_turned"), sem("y_made")
        y_stats_made, y_stats_seen, y_moments_made = sem("y_stats_made"), sem("y_stats_seen"), sem("y_moments_made")
        y_eps_added, y_rstd_made, y_normed = sem("y_eps_added"), sem("y_rstd_made"), sem("y_normed")
        y_turned, affine_made = sem("y_turned"), sem("affine_made")
        g_ready, gate_made = sem("g_ready"), sem("gate_made")
        z_made, z_hi_made, z_split = sem("z_made"), sem("z_hi_made"), sem("z_split")
        o_ready, residual = sem("o_ready"), sem("residual")
        stats_made, stats_seen, moments_made = sem("stats_made"), sem("stats_seen"), sem("moments_made")
        eps_added, rstd_made, normed = sem("eps_added"), sem("rstd_made"), sem("normed")
        block = stack.enter_context(nc.Block())

        def over_steps(eng, step, end):
            step(0, 0, 0, True)
            step(0, 1, 1, False)
            with eng.Fori(1, PAIRS) as i:
                for u in range(2):
                    step(i, 2 * i + u, u, False)
            end()

        def minus_two(i, c, u):
            return i - 1, c - 2, u

        @block.sync
        def _(sp):
            def load_weight(w):
                need(sp, w_split, w - 1)
                sp.dma_start(w_raw[:, w % 2], weights[w].rearrange("(t p) h -> p t h", p=P)
                             ).then_inc(w_loaded[w % 2], 16)

            def load_turned(c):
                need(sp, x_split, c)
                sp.dma_start(x_t[:], x_turned[:, bass.ds(c * CHUNK, CHUNK)].rearrange("(t p) n -> p t n", p=P)
                             ).then_inc(x_t_loaded, 16)

            load_weight(WV)
            load_turned(0)
            load_weight(WQ)
            with nc.allow_non_contiguous_dma(reason="short vectors, one channel for each partition"):
                for j in range(4):
                    sp.dma_start(decay_in[32 * j:32 * j + 32, :],
                                 beta.rearrange("(k j) -> j k", j=4)[j:j + 1, :].broadcast_to([32, KT])
                                 ).then_inc(vectors_loaded, 16)
                for source, column in ((ln_w, ln_w_col), (ln_b, ln_b_col)):
                    sp.dma_start(column[:], source.rearrange("(t p) -> p t", p=P)).then_inc(vectors_loaded, 16)

            def store(c, half):
                sp.wait_ge(normed, (c + 1) * TT)
                sp.dma_start(tokens_of(x_out, c), total[:, half]).then_inc(stored[half], 16)

            def step(i, c, u, front_only):
                if not (isinstance(c, int) and c == 0):
                    load_turned(c)
                need(sp, residual, (c - 1) * TT)
                sp.dma_start(x_tok[:, u], tokens_of(x_rows, c)).then_inc(x_loaded[u], 16)
                if isinstance(c, int) and c == 0:
                    load_weight(WG)
                    load_weight(WO)
                if not (isinstance(c, int) and c < 2):
                    store(c - 2, u)

            over_steps(sp, step, lambda: (store(CHUNKS - 2, 0), store(CHUNKS - 1, 1)))
            sp.wait_ge(stored[0], 16 * PAIRS)
            sp.wait_ge(stored[1], 16 * PAIRS)

        @block.gpsimd
        def _(pool):
            nc.gpsimd.memset(minus_half[:], -0.5).then_inc(constants_set, 1)
            nc.gpsimd.memset(eps[:], LN_EPS).then_inc(constants_set, 1)
            pool.wait_ge(constants_set, 2)

            def norm_scale(c, moments, moments_made, var_eps, eps_added, rstd, rstd_made, normed):
                pool.wait_ge(moments_made, (c + 1) * TT)
                need(pool, rstd_made, c)
                need(pool, normed, c * TT)
                nc.gpsimd.tensor_tensor(var_eps[:], moments[:, :, 1], eps[:], ALU.add).then_inc(eps_added, 1)
                pool.wait_ge(eps_added, c + 1)
                nc.gpsimd.tensor_tensor(rstd[:], var_eps[:], minus_half[:], ALU.pow).then_inc(rstd_made, 1)

            def result_scale(c):
                norm_scale(c, moments, moments_made, var_eps, eps_added, rstd, rstd_made, normed)

            def step(i, c, u, front_only):
                if not (isinstance(c, int) and c < 2):
                    result_scale(c - 2)
                norm_scale(c, y_moments, y_moments_made, y_var_eps, y_eps_added, y_rstd, y_rstd_made, y_normed)

            over_steps(pool, step, lambda: (result_scale(CHUNKS - 2), result_scale(CHUNKS - 1)))

        @block.scalar
        def _(act):
            def weight_high(w):
                act.wait_ge(w_loaded[w % 2], 16 * (w // 2 + 1))
                nc.scalar.copy(w_hi[:, w], w_raw[:, w % 2]).then_inc(w_hi_made, 1)

            def x_high(c):
                act.wait_ge(x_t_loaded, 16 * (c + 1))
                need(act, g_ready, c * KT)
                nc.scalar.copy(x_hi[:], x_t[:]).then_inc(x_hi_made, 1)

            def keep_q(c):
                for t in range(TT):
                    act.wait_ge(q_ready, c * TT + t + 1)
                    need(act, y_made, (c - 1) * TT + t + 1)
                    nc.scalar.copy(q_kept[:, t], tok_ps[:, t]).then_inc(q_out, 1)

            def scale_and_shift(c):
                for k in range(KT):
                    act.wait_ge(y_turned, c * KT + k + 1)
                    need(act, z_split, (c - 1) * KT + k + 1)
                    nc.scalar.activation(z[:, k], chan_ps[:, k], ACT.Identity, scale=ln_w_col[:, k:k + 1],
                                         bias=ln_b_col[:, k:k + 1]).then_inc(affine_made, 1)

            def z_high(c):
                for k in range(KT):
                    act.wait_ge(z_made, c * KT + k + 1)
                    need(act, o_ready, c * TT)
                    nc.scalar.copy(z_hi[:, k], z[:, k]).then_inc(z_hi_made, 1)

            def make_gate(c):
                for k in range(KT):
                    act.wait_ge(g_ready, c * KT + k + 1)
                    need(act, z_made, (c - 1) * KT + k + 1)
                    nc.scalar.activation(gate[:, k], chan_ps[:, k], ACT.Silu).then_inc(gate_made, 1)

            def back(c):
                scale_and_shift(c)
                z_high(c)

            def step(i, c, u, front_only):
                keep_q(c)
                if not front_only:
                    back(c - 1)
                make_gate(c)
                if not (isinstance(c, int) and c == CHUNKS - 1):
                    x_high(c + 1)

            weight_high(WV)
            x_high(0)
            weight_high(WQ)
            act.wait_ge(vectors_loaded, 16 * 6)
            nc.scalar.activation(decay[:], decay_in[:], ACT.Sigmoid).then_inc(decay_made, 1)
            weight_high(WG)
            weight_high(WO)
            step(0, 0, 0, True)
            step(0, 1, 1, False)
            with act.Fori(1, PAIRS - 1) as i:
                for u in range(2):
                    step(i, 2 * i + u, u, False)
            for u in range(2):
                step(PAIRS - 1, CHUNKS - 2 + u, u, False)
            back(CHUNKS - 1)

        @block.vector
        def _(dve):
            def weight_low(w):
                dve.wait_ge(w_hi_made, w + 1)
                nc.vector.tensor_tensor(w_lo[:, w], w_raw[:, w % 2], w_hi[:, w], ALU.subtract).then_inc(w_split, 1)

            def x_low(c):
                dve.wait_ge(x_hi_made, c + 1)
                nc.vector.tensor_tensor(x_lo[:], x_t[:], x_hi[:], ALU.subtract).then_inc(x_split, 1)

            def scan(c, u):
                for k in range(KT):
                    dve.wait_ge(v_ready, c * KT + k + 1)
                    need(dve, state_turned, (c - 1) * TT)
                    if u == 1:
                        dve.wait_ge(scanned, c * KT)
                    start = 0.0 if u == 0 else state[:, 0, k, CHUNK - 1:CHUNK]
                    nc.vector.tensor_tensor_scan(state[:, u, k], decay[:, k:k + 1].to_broadcast((P, CHUNK)),
                                                 chan_ps[:, k], start, ALU.mult, ALU.add).then_inc(scanned, 1)

            def make_y(c):
                for t in range(TT):
                    dve.wait_ge(state_turned, c * TT + t + 1)
                    need(dve, y_turned, c * KT)
                    nc.vector.tensor_tensor(y[:, t], tok_ps[:, t], q_kept[:, t], ALU.mult).then_inc(y_made, 1)

            def take_y_moments(c):
                need(dve, y_moments_made, c * TT)
                for t in range(TT):
                    dve.wait_ge(y_made, c * TT + t + 1)
                    nc.vector.bn_stats(y_stats[:, t], y[:, t]).then_inc(y_stats_made, 1)
                need(dve, y_normed, c * TT)
                dve.wait_ge(y_stats_made, (c + 1) * TT)
                dve.sem_inc(y_stats_seen, 1)
                for t in range(TT):
                    nc.vector.bn_aggr(y_moments[:, t], y_stats[:, t]).then_inc(y_moments_made, 1)

            def normalise_y(c):
                dve.wait_ge(y_rstd_made, c + 1)
                for t in range(TT):
                    nc.vector.tensor_scalar(y[:, t], y[:, t], y_moments[:, t, 0:1], y_rstd[:, t:t + 1],
                                            ALU.subtract, ALU.mult).then_inc(y_normed, 1)

            def make_z(c):
                for k in range(KT):
                    dve.wait_ge(affine_made, c * KT + k + 1)
                    dve.wait_ge(gate_made, c * KT + k + 1)
                    nc.vector.tensor_tensor(z[:, k], z[:, k], gate[:, k], ALU.mult).then_inc(z_made, 1)

            def z_low(c):
                for k in range(KT):
                    dve.wait_ge(z_hi_made, c * KT + k + 1)
                    nc.vector.tensor_tensor(z_lo[:, k], z[:, k], z_hi[:, k], ALU.subtract).then_inc(z_split, 1)

            def add_residual(i, c, u):
                dve.wait_ge(x_loaded[u], 16 * (i + 1))
                need(dve, stored[u], 16 * i)
                for t in range(TT):
                    dve.wait_ge(o_ready, c * TT + t + 1)
                    nc.vector.tensor_tensor(total[:, u, t], tok_ps[:, t], x_tok[:, u, t],
                                            ALU.add).then_inc(residual, 1)

            def take_moments(c, u):
                need(dve, moments_made, c * TT)
                for t in range(TT):
                    dve.wait_ge(residual, c * TT + t + 1)
                    nc.vector.bn_stats(stats[:, t], total[:, u, t]).then_inc(stats_made, 1)
                need(dve, normed, c * TT)
                dve.wait_ge(stats_made, (c + 1) * TT)
                dve.sem_inc(stats_seen, 1)
                for t in range(TT):
                    nc.vector.bn_aggr(moments[:, t], stats[:, t]).then_inc(moments_made, 1)

            def normalise(c, u):
                dve.wait_ge(rstd_made, c + 1)
                for t in range(TT):
                    nc.vector.tensor_scalar(total[:, u, t], total[:, u, t], moments[:, t, 0:1], rstd[:, t:t + 1],
                                            ALU.subtract, ALU.mult).then_inc(normed, 1)

            def step(i, c, u, front_only):
                finishing = not (isinstance(c, int) and c < 2)
                if finishing:
                    add_residual(*minus_two(i, c, u))
                    take_moments(c - 2, u)
                scan(c, u)
                if finishing:
                    normalise(c - 2, u)
                if not front_only:
                    make_z(c - 1)
                make_y(c)
                if not front_only:
                    z_low(c - 1)
                take_y_moments(c)
                normalise_y(c)
                if not (isinstance(c, int) and c == CHUNKS - 1):
                    x_low(c + 1)

            weight_low(WV)
            x_low(0)
            for w in (WQ, WG, WO):
                weight_low(w)
            dve.wait_ge(decay_made, 1)
            step(0, 0, 0, True)
            step(0, 1, 1, False)
            with dve.Fori(1, PAIRS - 1) as i:
                for u in range(2):
                    step(i, 2 * i + u, u, False)
            for u in range(2):
                step(PAIRS - 1, CHUNKS - 2 + u, u, False)
            add_residual(PAIRS - 1, CHUNKS - 2, 0)
            take_moments(CHUNKS - 2, 0)
            normalise(CHUNKS - 2, 0)
            make_z(CHUNKS - 1)
            z_low(CHUNKS - 1)
            add_residual(PAIRS - 1, CHUNKS - 1, 1)
            take_moments(CHUNKS - 1, 1)
            normalise(CHUNKS - 1, 1)

        @block.tensor
        def _(pe):
            PRODUCTS = ((0, 0), (0, 1), (1, 0))
            w_parts = (w_hi, w_lo)

            def to_channels(which, k_out, done):
                parts = (x_hi, x_lo)
                for k in range(KT):
                    for n, (a, b) in enumerate(PRODUCTS):
                        last = nc.tensor.matmul(chan_ps[:, k_out], w_parts[a][:, which, k, k_out * P:(k_out + 1) * P],
                                                parts[b][:, k], start=(k == 0 and n == 0),
                                                stop=(k == KT - 1 and n == 2))
                last.then_inc(done, 1)

            def to_tokens(which, parts, t, done):
                for k in range(KT):
                    for n, (a, b) in enumerate(PRODUCTS):
                        last = nc.tensor.matmul(tok_ps[:, t], parts[b][:, k, t * P:(t + 1) * P],
                                                w_parts[a][:, which, k], start=(k == 0 and n == 0),
                                                stop=(k == KT - 1 and n == 2))
                last.then_inc(done, 1)

            def turn_y(c, taken):
                pe.wait_ge(y_normed, (c + 1) * TT)
                for k in range(KT):
                    sem, per_chunk_before = taken
                    need(pe, sem, per_chunk_before * KT + k + 1)
                    for t in range(TT):
                        last = nc.tensor.transpose(chan_ps[:, k, t * P:(t + 1) * P], y[:, t, k * P:(k + 1) * P], ident)
                    last.then_inc(y_turned, 1)

            def output(c, wait):
                pe.wait_ge(z_split, (c + 1) * KT)
                for t in range(TT):
                    wait(t)
                    to_tokens(WO, (z_hi, z_lo), t, o_ready)

            def first_use(w, c):
                if isinstance(c, int) and c == 0:
                    pe.wait_ge(w_split, w + 1)

            def step(i, c, u, front_only):
                pe.wait_ge(x_split, c + 1)
                first_use(WV, c)
                for k in range(KT):
                    need(pe, gate_made, (c - 1) * KT + k + 1)
                    to_channels(WV, k, v_ready)
                first_use(WQ, c)
                for t in range(TT):
                    need(pe, residual, (c - 2) * TT + t + 1)
                    to_tokens(WQ, (x_hi, x_lo), t, q_ready)
                if not front_only:
                    turn_y(c - 1, (scanned, c))
                pe.wait_ge(scanned, (c + 1) * KT)
                for t in range(TT):
                    pe.wait_ge(q_out, c * TT + t + 1)
                    for k in range(KT):
                        last = nc.tensor.transpose(tok_ps[:, t, k * P:(k + 1) * P],
                                                   state[:, u, k, t * P:(t + 1) * P], ident)
                    last.then_inc(state_turned, 1)
                first_use(WO, c)
                for k in range(KT):
                    if front_only:
                        pe.wait_ge(scanned, (c + 1) * KT)
                    else:
                        pe.wait_ge(affine_made, (c - 1) * KT + k + 1)
                    to_channels(WG, k, g_ready)
                if not front_only:
                    output(c - 1, lambda t: pe.wait_ge(y_made, c * TT + t + 1))

            def end():
                turn_y(CHUNKS - 1, (gate_made, CHUNKS - 1))
                output(CHUNKS - 1, lambda t: pe.wait_ge(residual, (CHUNKS - 2) * TT + t + 1))

            over_steps(pe, step, end)


def ffn_phase(nc, tag, x_in, x_out, ident, w_gate, w_up, w_down, hidden_tiles,
              gate_function, gate_scale, up_scale, down_scale, hidden_type, beside=None,
              weight_sources=None):
    HT = hidden_tiles
    RING = 4
    LAG = 3

    with ExitStack() as stack:
        x_tok = stack.enter_context(nc.sbuf_tensor(tag + "x_tok", [P, 2, TT, D], F32))
        x_hi = stack.enter_context(nc.sbuf_tensor(tag + "x_hi", [P, 2, KT, CHUNK], F16))
        x_lo = stack.enter_context(nc.sbuf_tensor(tag + "x_lo", [P, 2, KT, CHUNK], F16))
        gated = stack.enter_context(nc.sbuf_tensor(tag + "gated", [P, 2, CHUNK], F32))
        hidden = stack.enter_context(nc.sbuf_tensor(tag + "hidden", [P, 2, CHUNK], F32))
        hid_hi = stack.enter_context(nc.sbuf_tensor(tag + "hid_hi", [P, RING, CHUNK], hidden_type))
        hid_lo = stack.enter_context(nc.sbuf_tensor(tag + "hid_lo", [P, RING, CHUNK], hidden_type))
        total = stack.enter_context(nc.sbuf_tensor(tag + "total", [P, 2, TT, D], F32))
        stats = stack.enter_context(nc.sbuf_tensor(tag + "stats", [P, TT, 6], F32))
        moments = stack.enter_context(nc.sbuf_tensor(tag + "moments", [P, TT, 2], F32))
        var_eps = stack.enter_context(nc.sbuf_tensor(tag + "var_eps", [P, TT], F32))
        rstd = stack.enter_context(nc.sbuf_tensor(tag + "rstd", [P, TT], F32))
        eps = stack.enter_context(nc.sbuf_tensor(tag + "eps", [P, TT], F32))
        minus_half = stack.enter_context(nc.sbuf_tensor(tag + "minus_half", [P, TT], F32))
        gate_ps = stack.enter_context(nc.psum_tensor(tag + "gate_ps", [P, 2, CHUNK], F32))
        up_ps = stack.enter_context(nc.psum_tensor(tag + "up_ps", [P, 2, CHUNK], F32))
        down_ps = stack.enter_context(nc.psum_tensor(tag + "down_ps", [P, TT, D], F32))
        x_loaded0 = stack.enter_context(nc.semaphore(tag + "x_loaded0"))
        x_loaded1 = stack.enter_context(nc.semaphore(tag + "x_loaded1"))
        turned = stack.enter_context(nc.semaphore(tag + "turned"))
        hi_made = stack.enter_context(nc.semaphore(tag + "hi_made"))
        split = stack.enter_context(nc.semaphore(tag + "split"))
        projected = stack.enter_context(nc.semaphore(tag + "projected"))
        gate_made = stack.enter_context(nc.semaphore(tag + "gate_made"))
        hidden_made = stack.enter_context(nc.semaphore(tag + "hidden_made"))
        hid_hi_made = stack.enter_context(nc.semaphore(tag + "hid_hi_made"))
        hid_lo_made = stack.enter_context(nc.semaphore(tag + "hid_lo_made"))
        hid_used = stack.enter_context(nc.semaphore(tag + "hid_used"))
        drained = stack.enter_context(nc.semaphore(tag + "drained"))
        residual = stack.enter_context(nc.semaphore(tag + "residual"))
        stats_made = stack.enter_context(nc.semaphore(tag + "stats_made"))
        stats_seen = stack.enter_context(nc.semaphore(tag + "stats_seen"))
        moments_made = stack.enter_context(nc.semaphore(tag + "moments_made"))
        half_set = stack.enter_context(nc.semaphore(tag + "half_set"))
        eps_added = stack.enter_context(nc.semaphore(tag + "eps_added"))
        rstd_made = stack.enter_context(nc.semaphore(tag + "rstd_made"))
        normed = stack.enter_context(nc.semaphore(tag + "normed"))
        stored0 = stack.enter_context(nc.semaphore(tag + "stored0"))
        stored1 = stack.enter_context(nc.semaphore(tag + "stored1"))
        weights_loaded = [stack.enter_context(nc.semaphore(tag + "weight%d_loaded" % n))
                          for n in range(3 if weight_sources else 0)]
        block = stack.enter_context(nc.Block())
        x_loaded = (x_loaded0, x_loaded1)
        stored = (stored0, stored1)

        def slot(u, j):
            return (u * (HT + 2) + 2 + j) % 2

        def turn_bank(u, k):
            ring = gate_ps if k % 2 == 0 else up_ps
            return ring[:, slot(u, k // 2 - 2), :]

        def slot_user(n, j):
            if j >= RING:
                return n - RING + 1
            before = j + RING * ((HT - 1 - j) // RING)
            return n - j - HT + before + 1

        @block.sync
        def _(sp):
            def pair(i, first, last):
                for u in range(2):
                    c = 2 * i + u
                    need(sp, residual, (c - 1) * TT)
                    sp.dma_start(x_tok[:, u], tokens_of(x_in, c)).then_inc(x_loaded[u], 16)
                    if weight_sources and first and u == 0:
                        for source, weight, done in zip(weight_sources, (w_gate, w_up, w_down), weights_loaded):
                            sp.dma_start(weight[:].rearrange("p t h -> p (t h)"), source).then_inc(done, 16)
                    if beside and first and u == 0:
                        beside.load(sp)
                    if not (first and u == 0):
                        sp.wait_ge(normed, c * TT)
                        sp.dma_start(tokens_of(x_out, c - 1), total[:, 1 - u]).then_inc(stored[1 - u], 16)
            over_pairs(sp, pair)
            sp.wait_ge(normed, CHUNKS * TT)
            sp.dma_start(tokens_of(x_out, CHUNKS - 1), total[:, 1]).then_inc(stored1, 16)
            sp.wait_ge(stored0, 16 * PAIRS)
            sp.wait_ge(stored1, 16 * PAIRS)

        @block.gpsimd
        def _(pool):
            nc.gpsimd.memset(minus_half[:], -0.5).then_inc(half_set, 1)
            nc.gpsimd.memset(eps[:], LN_EPS).then_inc(half_set, 1)
            pool.wait_ge(half_set, 2)

            def norm_scale(c):
                pool.wait_ge(moments_made, (c + 1) * TT)
                need(pool, rstd_made, c)
                need(pool, normed, c * TT)
                nc.gpsimd.tensor_tensor(var_eps[:], moments[:, :, 1], eps[:], ALU.add).then_inc(eps_added, 1)
                pool.wait_ge(eps_added, c + 1)
                nc.gpsimd.tensor_tensor(rstd[:], var_eps[:], minus_half[:], ALU.pow).then_inc(rstd_made, 1)

            over_pairs(pool, lambda i, first, last: (norm_scale(2 * i), norm_scale(2 * i + 1)))

        @block.scalar
        def _(act):
            def high_parts(c, u):
                for k in range(KT):
                    act.wait_ge(turned, c * KT + k + 1)
                    if k == 0:
                        need(act, projected, (c - 1) * HT)
                    nc.scalar.copy(x_hi[:, u, k], turn_bank(u, k)).then_inc(hi_made, 1)

            def hidden_high(c, u, j):
                n = c * HT + j
                act.wait_ge(hidden_made, n + 1)
                need(act, hid_used, slot_user(n, j))
                nc.scalar.copy(hid_hi[:, j % RING], hidden[:, (u * HT + j) % 2]).then_inc(hid_hi_made, 1)

            def pair(i, first, last):
                for u in range(2):
                    c = 2 * i + u
                    for j in range(HT):
                        n = c * HT + j
                        act.wait_ge(projected, n + 1)
                        need(act, hidden_made, n - 1)
                        scale = 1.0 if gate_scale is None else gate_scale[:, j:j + 1]
                        nc.scalar.activation(gated[:, (u * HT + j) % 2], gate_ps[:, slot(u, j)],
                                             gate_function, scale=scale).then_inc(gate_made, 1)
                        if j >= 1:
                            hidden_high(c, u, j - 1)
                        if beside and first and u == 1 and j == 1:
                            beside.gather_sums(act)
                        if beside and last and u == 0 and j >= 1:
                            beside.store(act, j - 1)
                    hidden_high(c, u, HT - 1)
                    if beside and last and u == 0:
                        beside.store(act, HT - 1)
                    if not (last and u == 1):
                        high_parts(c + 1, 1 - u)

            high_parts(0, 0)
            over_pairs(act, pair)
            if beside:
                beside.finish(act)

        @block.vector
        def _(dve):
            def low_parts(c, u):
                for k in range(KT):
                    dve.wait_ge(hi_made, c * KT + k + 1)
                    nc.vector.tensor_tensor(x_lo[:, u, k], turn_bank(u, k), x_hi[:, u, k],
                                            ALU.subtract).then_inc(split, 1)

            def hidden_low(c, u, j):
                dve.wait_ge(hid_hi_made, c * HT + j + 1)
                nc.vector.tensor_tensor(hid_lo[:, j % RING], hidden[:, (u * HT + j) % 2],
                                        hid_hi[:, j % RING], ALU.subtract).then_inc(hid_lo_made, 1)

            def drain(i, c, u):
                dve.wait_ge(hid_used, (c + 1) * HT)
                need(dve, stored[u], 16 * i)
                for t in range(TT):
                    if down_scale is None:
                        if t == 0:
                            dve.wait_ge(x_loaded[u], 16 * (i + 1))
                        nc.vector.tensor_tensor(total[:, u, t], down_ps[:, t], x_tok[:, u, t],
                                                ALU.add).then_inc(residual, 1)
                    else:
                        nc.vector.tensor_tensor(total[:, u, t], down_ps[:, t], down_scale,
                                                ALU.mult).then_inc(drained, 1)

            def add_input(i, c, u):
                if down_scale is None:
                    return
                dve.wait_ge(x_loaded[u], 16 * (i + 1))
                for t in range(TT):
                    dve.wait_ge(drained, c * TT + t + 1)
                    nc.vector.tensor_tensor(total[:, u, t], total[:, u, t], x_tok[:, u, t],
                                            ALU.add).then_inc(residual, 1)

            def take_stats(c, u):
                need(dve, moments_made, c * TT)
                for t in range(TT):
                    dve.wait_ge(residual, c * TT + t + 1)
                    nc.vector.bn_stats(stats[:, t], total[:, u, t]).then_inc(stats_made, 1)

            def take_moments(c):
                need(dve, normed, c * TT)
                dve.wait_ge(stats_made, (c + 1) * TT)
                dve.sem_inc(stats_seen, 1)
                for t in range(TT):
                    nc.vector.bn_aggr(moments[:, t], stats[:, t]).then_inc(moments_made, 1)

            def normalise(c, u):
                dve.wait_ge(rstd_made, c + 1)
                for t in range(TT):
                    nc.vector.tensor_scalar(total[:, u, t], total[:, u, t], moments[:, t, 0:1], rstd[:, t:t + 1],
                                            ALU.subtract, ALU.mult).then_inc(normed, 1)

            def finish(i, c, u, step):
                if step == 0:
                    drain(i, c, u)
                elif step == 1:
                    add_input(i, c, u)
                elif step == 2:
                    take_stats(c, u)
                elif step == 3:
                    take_moments(c)
                elif step == 6:
                    normalise(c, u)

            def pair(i, first, last):
                for u in range(2):
                    c = 2 * i + u
                    for j in range(HT):
                        if not (first and u == 0):
                            finish(i - 1 + u, c - 1, 1 - u, j)
                        n = c * HT + j
                        dve.wait_ge(gate_made, n + 1)
                        need(dve, hid_lo_made, n - 1)
                        m = (u * HT + j) % 2
                        if up_scale is None:
                            nc.vector.tensor_tensor(hidden[:, m], up_ps[:, slot(u, j)], gated[:, m],
                                                    ALU.mult).then_inc(hidden_made, 1)
                        else:
                            nc.vector.scalar_tensor_tensor(
                                out=hidden[:, m], in0=up_ps[:, slot(u, j)], scalar=up_scale[:, j:j + 1],
                                in1=gated[:, m], op0=ALU.mult, op1=ALU.mult).then_inc(hidden_made, 1)
                        if j >= 1:
                            hidden_low(c, u, j - 1)
                        if beside and first and u == 0:
                            beside.sum_piece(dve, j)
                        if beside and first and u == 1 and j == 0:
                            beside.sum_matrices(dve)
                        if beside and first and u == 1 and j == 5:
                            beside.make_gamma(dve)
                        if beside and last and u == 0:
                            beside.quantise(dve, j)
                    hidden_low(c, u, HT - 1)
                    if not (last and u == 1):
                        low_parts(c + 1, 1 - u)

            low_parts(0, 0)
            over_pairs(dve, pair)
            for step in range(7):
                finish(PAIRS - 1, CHUNKS - 1, 1, step)

        @block.tensor
        def _(pe):
            def turn(i, c, u):
                pe.wait_ge(x_loaded[u], 16 * (i + 1))
                for k in range(KT):
                    need(pe, gate_made if k % 2 == 0 else hidden_made, (c - 1) * HT + HT - 1 + k // 2)
                    for t in range(TT):
                        last = nc.tensor.transpose(turn_bank(u, k)[:, t * P:(t + 1) * P],
                                                   x_tok[:, u, t, k * P:(k + 1) * P], ident)
                    last.then_inc(turned, 1)

            def project(c, u, j):
                n = c * HT + j
                if j == 0:
                    pe.wait_ge(split, (c + 1) * KT)
                for n_weight, (weight, bank, taken) in enumerate(((w_gate, gate_ps, gate_made),
                                                                  (w_up, up_ps, hidden_made))):
                    if weight_sources and isinstance(c, int) and c == 0 and j == 0:
                        pe.wait_ge(weights_loaded[n_weight], 16)
                    if j >= 2:
                        pe.wait_ge(taken, n - 1)
                    for k in range(KT):
                        for part in (x_hi, x_lo):
                            last = nc.tensor.matmul(bank[:, slot(u, j)], weight[:, k, j * P:(j + 1) * P],
                                                    part[:, u, k], start=(k == 0 and part is x_hi),
                                                    stop=(k == KT - 1 and part is x_lo))
                last.then_inc(projected, 1)

            def down(c, j):
                pe.wait_ge(hid_lo_made, c * HT + j + 1)
                if weight_sources and isinstance(c, int) and c == 0 and j == 0:
                    pe.wait_ge(weights_loaded[2], 16)
                for t in range(TT):
                    if j == 0:
                        need(pe, residual if down_scale is None else drained, (c - 1) * TT + t + 1)
                    for part in (hid_hi, hid_lo):
                        last = nc.tensor.matmul(down_ps[:, t], part[:, j % RING, t * P:(t + 1) * P], w_down[:, j],
                                                start=(j == 0 and part is hid_hi),
                                                stop=(j == HT - 1 and part is hid_lo))
                last.then_inc(hid_used, 1)

            def pair(i, first, last):
                for u in range(2):
                    c = 2 * i + u
                    for j in range(HT):
                        project(c, u, j)
                        if j >= LAG:
                            down(c, j - LAG)
                    if not (last and u == 1):
                        turn(i + u, c + 1, 1 - u)
                    for j in range(HT - LAG, HT):
                        down(c, j)

            turn(0, 0, 0)
            over_pairs(pe, pair)


HEADS = 16
HEAD = D // HEADS
RANK = 16
LORA_SCALE = 8.0 / RANK
SOFTMAX_SCALE = HEAD ** -0.5
WEIGHT_LIFT = 256.0
QUERY_LIFT = 32.0
MAX_LIFT = 2.0 ** 14


def lora_weights(nc, ident, weights, a_turned, b_rows, biases, w_hi, w_lo, bias_cols, bias_rows, exp_scale,
                 out_scale):
    tag = "lora_"
    Q, K, V, O = range(4)
    with ExitStack() as stack:
        def sbuf(name, shape, dtype=F32):
            return stack.enter_context(nc.sbuf_tensor(tag + name, shape, dtype))

        def sem(name):
            return stack.enter_context(nc.semaphore(tag + name))

        raw = sbuf("raw", [P, 4, KT, D])
        a_sb = sbuf("a_sb", [RANK, 4, D])
        b_sb = sbuf("b_sb", [RANK, 4, D])
        largest = sbuf("largest", [P, 2, 4])
        both = sbuf("both", [P, 4])
        top = sbuf("top", [4, 1])
        top_row = sbuf("top_row", [4, P])
        power = sbuf("power", [P, 4])
        inverse = sbuf("inverse", [P, 4])
        lift = sbuf("lift", [P, 4])
        update = stack.enter_context(nc.psum_tensor(tag + "update", [P, KT, D], F32))
        turned = stack.enter_context(nc.psum_tensor(tag + "turned", [4, P], F32))
        spread = stack.enter_context(nc.psum_tensor(tag + "spread", [P, 4], F32))
        loaded = [sem("loaded%d" % n) for n in range(4)]
        vectors_loaded, chain = sem("vectors_loaded"), sem("chain")
        updated, added, maxed, max_turned, top_made = (sem("updated"), sem("added"), sem("maxed"),
                                                       sem("max_turned"), sem("top_made"))
        top_spread, lift_made, hi_made, lo_made = sem("top_spread"), sem("lift_made"), sem("hi_made"), sem("lo_made")
        block = stack.enter_context(nc.Block())

        @block.sync
        def _(sp):
            for n in range(4):
                sp.dma_start(a_sb[:, n], a_turned[n]).then_inc(loaded[n], 16)
                sp.dma_start(b_sb[:, n], b_rows[n]).then_inc(loaded[n], 16)
                sp.dma_start(raw[:, n], weights[n].rearrange("(t p) h -> p t h", p=P)).then_inc(loaded[n], 16)
            with nc.allow_non_contiguous_dma(reason="short vectors, one channel for each partition"):
                for n in (Q, K):
                    sp.dma_start(bias_cols[:, n], biases[n].rearrange("(t p) -> p t", p=P)).then_inc(vectors_loaded, 16)
            for n in (V, O):
                sp.dma_start(bias_rows[:, n - V], biases[n].rearrange("(o n) -> o n", o=1).partition_broadcast(P)
                             ).then_inc(vectors_loaded, 16)

        @block.tensor
        def _(pe):
            for n in range(4):
                pe.wait_ge(loaded[n], 48)
                for k in range(KT):
                    need(pe, added, (n - 1) * KT + k + 1)
                    nc.tensor.matmul(update[:, k], b_sb[:, n, k * P:(k + 1) * P], a_sb[:, n],
                                     start=True, stop=True).then_inc(updated, 1)
            pe.wait_ge(maxed, 9)
            nc.tensor.transpose(turned[:], both[:], ident).then_inc(max_turned, 1)
            pe.wait_ge(top_made, 2)
            nc.tensor.matmul(spread[:], top_row[:], ident[0:4, 0:4], start=True, stop=True).then_inc(top_spread, 1)

        @block.scalar
        def _(act):
            act.wait_ge(lift_made, 1)
            for n in range(4):
                nc.scalar.activation(w_hi[:, n], raw[:, n], ACT.Copy, scale=lift[:, n:n + 1]).then_inc(hi_made, 1)

        @block.vector
        def _(dve):
            for n in range(4):
                for k in range(KT):
                    dve.wait_ge(updated, n * KT + k + 1)
                    nc.vector.scalar_tensor_tensor(out=raw[:, n, k], in0=update[:, k], scalar=LORA_SCALE,
                                                   in1=raw[:, n, k], op0=ALU.mult, op1=ALU.add).then_inc(added, 1)
                dve.wait_ge(added, (n + 1) * KT)
                nc.vector.tensor_reduce(largest[:, 0, n:n + 1], raw[:, n], AX.XY, ALU.max,
                                        apply_absolute_value=True).then_inc(maxed, 1)
            dve.wait_ge(vectors_loaded, 64)
            for n in range(4):
                bias = bias_cols[:, n] if n < V else bias_rows[:, n - V]
                nc.vector.tensor_reduce(largest[:, 1, n:n + 1], bias, AX.X, ALU.max,
                                        apply_absolute_value=True).then_inc(maxed, 1)
            dve.wait_ge(maxed, 8)
            nc.vector.tensor_tensor(both[:], largest[:, 0], largest[:, 1], ALU.max).then_inc(maxed, 1)
            dve.wait_ge(max_turned, 1)
            nc.vector.tensor_reduce(top[:], turned[:], AX.X, ALU.max).then_inc(top_made, 1)
            dve.wait_ge(top_made, 1)
            nc.vector.tensor_copy(top_row[:], top[:].to_broadcast((4, P))).then_inc(top_made, 1)
            dve.wait_ge(top_spread, 1)
            nc.vector.tensor_scalar(power[:], spread[:], 2.0 ** -101, None, ALU.max).then_inc(chain, 1)
            dve.wait_ge(chain, 1)
            nc.vector.tensor_scalar(power[:].bitcast(U32), power[:].bitcast(U32), 0x7F800000, None,
                                    ALU.bitwise_and).then_inc(chain, 1)
            dve.wait_ge(chain, 2)
            nc.vector.tensor_scalar(power[:], power[:], 2.0, None, ALU.mult).then_inc(chain, 1)
            dve.wait_ge(chain, 3)
            nc.vector.reciprocal(inverse[:], power[:]).then_inc(chain, 1)
            dve.wait_ge(chain, 4)
            nc.vector.tensor_scalar(lift[:], inverse[:], WEIGHT_LIFT, None, ALU.mult).then_inc(lift_made, 1)
            nc.vector.tensor_scalar(bias_cols[:, Q], bias_cols[:, Q], inverse[:, Q:Q + 1], QUERY_LIFT,
                                    ALU.mult, ALU.mult).then_inc(chain, 1)
            nc.vector.tensor_scalar(bias_cols[:, K], bias_cols[:, K], inverse[:, K:K + 1], None,
                                    ALU.mult).then_inc(chain, 1)
            nc.vector.tensor_scalar(bias_rows[:, 0], bias_rows[:, 0], inverse[:, V:V + 1], None,
                                    ALU.mult).then_inc(chain, 1)
            nc.vector.tensor_scalar(exp_scale[:], power[:, Q:Q + 1], power[:, K:K + 1], SOFTMAX_SCALE / QUERY_LIFT,
                                    ALU.mult, ALU.mult).then_inc(chain, 1)
            nc.vector.tensor_scalar(out_scale[:], power[:, V:V + 1], power[:, O:O + 1],
                                    1.0 / (QUERY_LIFT * WEIGHT_LIFT), ALU.mult, ALU.mult).then_inc(chain, 1)
            dve.wait_ge(lift_made, 1)
            for n in range(4):
                dve.wait_ge(hi_made, n + 1)
                flat = "p t h -> p (t h)"
                nc.vector.scalar_tensor_tensor(out=w_lo[:, n].rearrange(flat), in0=raw[:, n].rearrange(flat),
                                               scalar=lift[:, n:n + 1], in1=w_hi[:, n].rearrange(flat),
                                               op0=ALU.mult, op1=ALU.subtract).then_inc(lo_made, 1)
            dve.wait_ge(lo_made, 4)
            dve.wait_ge(chain, 9)


def attention_phase(nc, x_in, x_out, ident, ones, w_hi, w_lo, bias_cols, bias_rows, exp_scale, out_scale):
    tag = "att_"
    WV, WO = 2, 3
    GROUPS = KT
    STEPS = BATCH * GROUPS
    G_HEADS = P // HEAD
    KEY_TILES = SEQ // P
    HALVES = SEQ // CHUNK
    PAIR = 2
    UNITS = HALVES * KEY_TILES * G_HEADS // PAIR
    HALF_UNITS = UNITS // HALVES
    MAXES = G_HEADS * KEY_TILES * HALVES
    ROWS = 3 * HEAD + 2
    PROBS = 4
    POOLED = 4
    TILES = SEQ // P
    STACK_DMAS = 6 * G_HEADS
    LEAD = -1
    PROJECTIONS = ((10, 12, 14, 16), (LEAD, 1, 2, 4), (2, 3, 4, 5), (LEAD, 1, 2, 4))
    PIECES = 4
    NORM_UNITS = (8, 10)

    with ExitStack() as stack:
        def sbuf(name, shape, dtype=F32):
            return stack.enter_context(nc.sbuf_tensor(tag + name, shape, dtype))

        def psum(name, shape):
            return stack.enter_context(nc.psum_tensor(tag + name, shape, F32))

        def sem(name):
            return stack.enter_context(nc.semaphore(tag + name))

        x_tok = sbuf("x_tok", [P, 2, TT, D])
        x_hi = sbuf("x_hi", [P, KT, SEQ], F16)
        x_lo = sbuf("x_lo", [P, KT, SEQ], F16)
        v = sbuf("v", [P, KEY_TILES, D])
        queries = sbuf("queries", [ROWS, 2, G_HEADS, SEQ], F16)
        keys = sbuf("keys", [ROWS, 2, G_HEADS, SEQ], F16)
        qk_full = sbuf("qk_full", [P, 2, CHUNK])
        qk_hi = sbuf("qk_hi", [P, 2, 2, SEQ], F16)
        qk_lo = sbuf("qk_lo", [P, 2, 2, SEQ], F16)
        maxes = sbuf("maxes", [P, MAXES // HALVES, HALVES])
        row_max = sbuf("row_max", [P, MAXES // HALVES])
        max_rows = sbuf("max_rows", [MAXES // HALVES, 2, P], F16)
        probs = sbuf("probs", [P, PROBS, PAIR, CHUNK])
        prob_sums = sbuf("prob_sums", [P, G_HEADS, CHUNK])
        mixed = sbuf("mixed", [P, 2, CHUNK])
        recip = sbuf("recip", [P, 2, CHUNK])
        z = sbuf("z", [P, 2, CHUNK])
        z_hi = sbuf("z_hi", [P, GROUPS, SEQ], F16)
        z_lo = sbuf("z_lo", [P, GROUPS, SEQ], F16)
        total = sbuf("total", [P, 2, TT, D])
        stats = sbuf("stats", [P, 2, TT, 6])
        moments = sbuf("moments", [P, 2, TT, 2])
        var_eps = sbuf("var_eps", [P, 2, TT])
        rstd = sbuf("rstd", [P, 2, TT])
        minus_half = sbuf("minus_half", [P, TT])
        eps = sbuf("eps", [P, TT])
        score_ps = psum("score_ps", [P, 2, PAIR, CHUNK])
        aux_ps = psum("aux_ps", [P, 2, CHUNK])
        mix_ps = psum("mix_ps", [P, CHUNK])
        sum_ps = psum("sum_ps", [P, CHUNK])

        constants_set, key_ones_set = sem("constants_set"), sem("key_ones_set")
        rows_loaded = (sem("rows_loaded0"), sem("rows_loaded1"))
        skip_loaded = (sem("skip_loaded0"), sem("skip_loaded1"))
        stored = (sem("stored0"), sem("stored1"))
        x_turned, x_hi_made, x_split = sem("x_turned"), sem("x_hi_made"), sem("x_split")
        v_ready, v_made = sem("v_ready"), sem("v_made")
        qk_ready, qk_full_made, qk_hi_made, qk_split = (sem("qk_ready"), sem("qk_full_made"), sem("qk_hi_made"),
                                                        sem("qk_split"))
        buffer_seen = sem("buffer_seen")
        stacked = (sem("stacked0"), sem("stacked1"))
        m_ready, maxed, row_max_made = sem("m_ready"), sem("maxed"), sem("row_max_made")
        rows_turned, rows_made, rows_split, rows_stacked = (sem("rows_turned"), sem("rows_made"), sem("rows_split"),
                                                            sem("rows_stacked"))
        scored, exp_made, pooled, weighed = sem("scored"), sem("exp_made"), sem("pooled"), sem("weighed")
        mix_kept, recip_made, z_made, z_hi_made, z_split = (sem("mix_kept"), sem("recip_made"), sem("z_made"),
                                                            sem("z_hi_made"), sem("z_split"))
        skip_biased, o_ready, residual = sem("skip_biased"), sem("o_ready"), sem("residual")
        stats_made, stats_seen, moments_made = sem("stats_made"), sem("stats_seen"), sem("moments_made")
        eps_added, rstd_made, normed = sem("eps_added"), sem("rstd_made"), sem("normed")
        block = stack.enter_context(nc.Block())

        def is_last(b):
            return isinstance(b, int) and b == BATCH - 1

        def is_first(b):
            return isinstance(b, int) and b == 0

        def over_batches(eng, body):
            body(0)
            with eng.Fori(1, BATCH - 1) as b:
                body(b)
            body(BATCH - 1)

        def unit_work(b, g):
            work = {e: [] for e in range(LEAD, UNITS)}
            if g == 0:
                if not is_first(b):
                    for t in range(TILES):
                        work[LEAD if t < TILES // 2 else 1].append(("v", t))
                        work[5 + t // 2].append(("o", t))
            if g == 2 and not is_last(b):
                for t in range(2 * KT):
                    work[LEAD if t < KT else 1].append(("t", t))
            if g > 0 and not (is_last(b) and g >= GROUPS - 2):
                for t in range(4):
                    work[PROJECTIONS[g][t]].append(("q", t))
            if not (is_last(b) and g == GROUPS - 1):
                places = []
                for e in range(8, UNITS - 1):
                    places += [e] * (2 if e % 2 == 0 else 5 if (e // 2 - 1) % KEY_TILES >= POOLED else 4)
                for m in range(MAXES):
                    work[places[m * len(places) // MAXES]].append(("m", m))
            if g == 0:
                for t in range(4):
                    work[PROJECTIONS[g][t]].append(("q", t))
            return work

        before_all = [(-1, 0, 0, "t", t) for t in range(2 * KT)]
        before_all += [(-1, n + 2, n - 2, "q", t) for n in range(2) for t in range(4)]
        before_all += [(0, 0, 0, "v", t) for t in range(TILES // 2)]
        for t in range(MAXES):
            before_all.append((0, -1, -1, "m", t))
            if t % (2 * MAXES // TILES) == 0:
                before_all.append((0, 0, 0, "v", TILES // 2 + t // (2 * MAXES // TILES)))
        before_all.append((0, -1, -1, "r", 0))

        @block.sync
        def _(sp):
            def load_rows(b, u):
                need(sp, x_turned, b * 2 * KT)
                need(sp, residual, (b - 2) * TILES + (u + 1) * TT)
                sp.dma_start(x_tok[:, u], tokens_of(x_in, b * HALVES + u)).then_inc(rows_loaded[u], 16)

            def load_skip(b, u):
                if is_last(b):
                    sp.wait_ge(residual, (b - 1) * TILES + (u + 1) * TT)
                else:
                    sp.wait_ge(x_turned, (b + 2) * 2 * KT)
                sp.dma_start(x_tok[:, u], tokens_of(x_in, b * HALVES + u)).then_inc(skip_loaded[u], 16)

            def stack_step(n, buffer):
                need(sp, scored, (n - 1) * UNITS)
                sp.sem_inc(buffer_seen, 1)
                for which, target, parts in ((0, queries, (qk_hi, qk_lo, qk_hi)), (1, keys, (qk_hi, qk_hi, qk_lo))):
                    sp.wait_ge(qk_split, 4 * n + 2 * which + 2)
                    for row, part in enumerate(parts):
                        for j in range(G_HEADS):
                            sp.dma_start(target[row * HEAD:(row + 1) * HEAD, buffer, j, :],
                                         part[j * HEAD:(j + 1) * HEAD, buffer, which, :]).then_inc(stacked[buffer], 16)

            def stack_max(n, buffer):
                for part, made in enumerate((rows_made, rows_split)):
                    sp.wait_ge(made, n + 1)
                    row = 3 * HEAD + part
                    sp.dma_start(queries[row:row + 1, buffer].rearrange("o j (t p) -> o (j t) p", p=P),
                                 max_rows[:, part]).then_inc(rows_stacked, 16)

            def store(b, u):
                sp.wait_ge(normed, b * TILES + (u + 1) * TT)
                sp.dma_start(tokens_of(x_out, b * HALVES + u), total[:, u]).then_inc(stored[u], 16)

            for u in range(HALVES):
                sp.sem_inc(stored[u], 16)
                load_rows(0, u)
            stack_step(0, 0)
            stack_step(1, 1)
            stack_max(0, 0)

            def body(b):
                for g in range(GROUPS):
                    n = b * GROUPS + g
                    if not (is_first(b) and g == 0) and not (is_last(b) and g == GROUPS - 1):
                        stack_step(n + 1, (g + 1) % 2)
                    if g == 0 and not is_first(b):
                        for u in range(HALVES):
                            store(b - 1, u)
                    if g == 1 and not is_last(b):
                        for u in range(HALVES):
                            load_rows(b + 1, u)
                    if g == GROUPS - 1:
                        for u in range(HALVES):
                            load_skip(b, u)
                    if not (is_last(b) and g == GROUPS - 1):
                        stack_max(n + 1, (g + 1) % 2)

            over_batches(sp, body)
            for u in range(HALVES):
                store(BATCH - 1, u)
                sp.wait_ge(stored[u], 16 * (BATCH + 1))

        @block.gpsimd
        def _(pool):
            nc.gpsimd.memset(minus_half[:], -0.5).then_inc(constants_set, 1)
            nc.gpsimd.memset(eps[:], LN_EPS).then_inc(constants_set, 1)
            pool.wait_ge(constants_set, 2)
            nc.gpsimd.memset(keys[3 * HEAD:ROWS, :, :, :], MAX_LIFT).then_inc(key_ones_set, 1)
            pool.wait_ge(key_ones_set, 1)

            def sum_probs(n, unit):
                kt, pair = (unit % HALF_UNITS) // 2, unit % 2
                half = n * HALVES + unit // HALF_UNITS
                sums = prob_sums[:, PAIR * pair:PAIR * pair + PAIR]
                pool.wait_ge(exp_made, n * UNITS + unit + 1)
                if kt == 1:
                    need(pool, weighed, half * KEY_TILES - KEY_TILES + POOLED + 1)
                    nc.gpsimd.tensor_tensor(sums, probs[:, (unit - 2) % PROBS], probs[:, unit % PROBS],
                                            ALU.add).then_inc(pooled, 1)
                else:
                    pool.wait_ge(pooled, half * 2 * (POOLED - 1) + 2 * (kt - 2) + pair + 1)
                    nc.gpsimd.tensor_tensor(sums, sums, probs[:, unit % PROBS], ALU.add).then_inc(pooled, 1)

            def z_low(n, half, g):
                pool.wait_ge(z_hi_made, n * HALVES + half + 1)
                at = slice(half * CHUNK, (half + 1) * CHUNK)
                nc.gpsimd.tensor_tensor(z_lo[:, g, at], z[:, half], z_hi[:, g, at], ALU.subtract).then_inc(z_split, 1)

            def add_bias(b, t):
                pool.wait_ge(skip_loaded[t // TT], 16 * (b + 1))
                rows = x_tok[:, t // TT, t % TT]
                nc.gpsimd.tensor_tensor(rows, rows, bias_rows[:, 1], ALU.add).then_inc(skip_biased, 1)

            def norm_scale(b, u):
                c = b * HALVES + u
                pool.wait_ge(moments_made, (c + 1) * TT)
                nc.gpsimd.tensor_tensor(var_eps[:, u], moments[:, u, :, 1], eps[:], ALU.add).then_inc(eps_added, 1)
                pool.wait_ge(eps_added, c + 1)
                nc.gpsimd.tensor_tensor(rstd[:, u], var_eps[:, u], minus_half[:], ALU.pow).then_inc(rstd_made, 1)

            def body(b):
                for g in range(GROUPS):
                    n = b * GROUPS + g
                    for unit in range(UNITS):
                        if unit == (3 if g == 0 else 5) and not (is_first(b) and g == 0):
                            z_low(n - 1, 1, (g - 1) % GROUPS)
                        if unit == HALF_UNITS + 9:
                            z_low(n, 0, g)
                        kt = (unit % HALF_UNITS) // 2
                        if 1 <= kt < POOLED:
                            sum_probs(n, unit)
                        if g == 0 and not is_first(b) and unit in NORM_UNITS:
                            norm_scale(b - 1, NORM_UNITS.index(unit))
                        if g == GROUPS - 1 and 8 <= unit < 8 + TILES:
                            add_bias(b, unit - 8)

            over_batches(pool, body)
            z_low(STEPS - 1, 1, GROUPS - 1)
            for u in range(HALVES):
                norm_scale(BATCH - 1, u)

        @block.scalar
        def _(act):
            def aux(b, g, n, kind, t, bank):
                if kind == "t":
                    half, k = t // KT, t % KT
                    act.wait_ge(x_turned, (b + 1) * 2 * KT + t + 1)
                    nc.scalar.copy(x_hi[:, k, half * CHUNK:(half + 1) * CHUNK], aux_ps[:, bank]).then_inc(x_hi_made, 1)
                elif kind == "q":
                    which, half = t // 2, t % 2
                    m = n + 2
                    act.wait_ge(qk_ready, 4 * m + t + 1)
                    need(act, qk_split, 4 * m + t - 1)
                    lift = QUERY_LIFT / WEIGHT_LIFT if which == 0 else 1.0 / WEIGHT_LIFT
                    group = (g + 2) % GROUPS
                    nc.scalar.activation(qk_full[:, t % 2], aux_ps[:, bank], ACT.Identity, scale=lift,
                                         bias=bias_cols[:, which, group:group + 1]).then_inc(qk_full_made, 1)
                    act.wait_ge(qk_full_made, 4 * m + t + 1)
                    if not (isinstance(m, int) and m < 2):
                        act.wait_ge(stacked[g % 2], (b * 2 + g // 2 + 1) * STACK_DMAS * 16)
                    nc.scalar.copy(qk_hi[:, g % 2, which, half * CHUNK:(half + 1) * CHUNK],
                                   qk_full[:, t % 2]).then_inc(qk_hi_made, 1)

            def exp(n, unit):
                e = n * UNITS + unit
                tiles = n * HALVES * KEY_TILES + unit // 2
                act.wait_ge(scored, e + 1)
                need(act, weighed, tiles - 1)
                kt = (unit % HALF_UNITS) // 2
                if 2 <= kt < POOLED + 2:
                    half = n * HALVES + unit // HALF_UNITS
                    done = half * 2 * (POOLED - 1) + 2 * max(kt - 3, 0) + unit % 2 + 1
                    act.wait_ge(pooled, done)
                nc.scalar.activation(probs[:, unit % PROBS], score_ps[:, unit % 2], ACT.Exp,
                                     scale=exp_scale[:, 0:1]).then_inc(exp_made, 1)

            def keep_mix(n, half):
                h = n * HALVES + half
                act.wait_ge(weighed, (h + 1) * KEY_TILES)
                need(act, z_made, h - 1)
                nc.scalar.copy(mixed[:, half], mix_ps[:]).then_inc(mix_kept, 1)

            def z_high(n, half, g):
                h = n * HALVES + half
                act.wait_ge(z_made, h + 1)
                nc.scalar.copy(z_hi[:, g, half * CHUNK:(half + 1) * CHUNK], z[:, half]).then_inc(z_hi_made, 1)

            def max_rows_out(n, bank):
                act.wait_ge(rows_turned, n + 1)
                need(act, rows_stacked, 32 * n)
                nc.scalar.mul(max_rows[:, 0], aux_ps[0:MAXES // HALVES, bank, 0:P], 1.0 / MAX_LIFT
                              ).then_inc(rows_made, 1)

            for i, tile_before in enumerate(before_all[:-1]):
                aux(*tile_before, (i + 1) % 2)
            max_rows_out(0, len(before_all) % 2)

            def body(b):
                for g in range(GROUPS):
                    n = b * GROUPS + g
                    work = unit_work(b, g)
                    position = 0
                    for unit in range(LEAD, UNITS):
                        if unit != LEAD:
                            exp(n, unit)
                        if unit == HALF_UNITS + 1:
                            keep_mix(n, 0)
                        if unit == (2 if g == 0 else 4) and not (is_first(b) and g == 0):
                            z_high(n - 1, 1, (g - 1) % GROUPS)
                        if unit == HALF_UNITS + 8:
                            if g == 0 and not is_first(b):
                                act.wait_ge(o_ready, b * TILES)
                            z_high(n, 0, g)
                        for kind, t in work[unit]:
                            aux(b, g, n, kind, t, (g + position) % 2)
                            position += 1
                    if not (is_last(b) and g == GROUPS - 1):
                        max_rows_out(n + 1, (g + position) % 2)
                    keep_mix(n, 1)

            over_batches(act, body)
            z_high(STEPS - 1, 1, GROUPS - 1)

        @block.vector
        def _(dve):
            def aux(b, g, n, kind, t, bank):
                if kind == "t":
                    half, k = t // KT, t % KT
                    at = slice(half * CHUNK, (half + 1) * CHUNK)
                    dve.wait_ge(x_hi_made, (b + 1) * 2 * KT + t + 1)
                    nc.vector.tensor_tensor(x_lo[:, k, at], aux_ps[:, bank], x_hi[:, k, at],
                                            ALU.subtract).then_inc(x_split, 1)
                elif kind == "q":
                    which, half = t // 2, t % 2
                    at = slice(half * CHUNK, (half + 1) * CHUNK)
                    dve.wait_ge(qk_hi_made, 4 * (n + 2) + t + 1)
                    nc.vector.tensor_tensor(qk_lo[:, g % 2, which, at], qk_full[:, t % 2], qk_hi[:, g % 2, which, at],
                                            ALU.subtract).then_inc(qk_split, 1)
                elif kind == "v":
                    dve.wait_ge(v_ready, b * TILES + t + 1)
                    nc.vector.scalar_tensor_tensor(out=v[:, t], in0=aux_ps[:, bank], scalar=1.0 / WEIGHT_LIFT,
                                                   in1=bias_rows[:, 0], op0=ALU.mult, op1=ALU.add
                                                   ).then_inc(v_made, 1)
                elif kind == "o":
                    u, tt = t // TT, t % TT
                    row = (b - 1) * TILES + t
                    if tt == 0:
                        dve.wait_ge(stored[u], 16 * b)
                    dve.wait_ge(skip_biased, row + 1)
                    dve.wait_ge(o_ready, row + 1)
                    nc.vector.scalar_tensor_tensor(out=total[:, u, tt], in0=aux_ps[:, bank], scalar=out_scale[:, 0:1],
                                                   in1=x_tok[:, u, tt], op0=ALU.mult, op1=ALU.add
                                                   ).then_inc(residual, 1)
                    dve.wait_ge(residual, row + 1)
                    nc.vector.bn_stats(stats[:, u, tt], total[:, u, tt]).then_inc(stats_made, 1)
                    if tt == TT - 1:
                        dve.wait_ge(stats_made, row + 1)
                        dve.sem_inc(stats_seen, 1)
                        for tt in range(TT):
                            nc.vector.bn_aggr(moments[:, u, tt], stats[:, u, tt]).then_inc(moments_made, 1)
                elif kind == "m":
                    tile = (n + 1) * MAXES + t
                    dve.wait_ge(m_ready, tile + 1)
                    if t == 0:
                        need(dve, row_max_made, n + 1)
                    nc.vector.tensor_reduce(maxes[:, t // HALVES, t % HALVES:t % HALVES + 1], aux_ps[:, bank],
                                            AX.X, ALU.max).then_inc(maxed, 1)

            def combine(n):
                dve.wait_ge(maxed, (n + 1) * MAXES)
                need(dve, rows_turned, n)
                nc.vector.tensor_reduce(row_max[:], maxes[:], AX.X, ALU.max, negate=True).then_inc(row_max_made, 1)

            def max_rows_low(n, bank):
                dve.wait_ge(rows_made, n + 1)
                nc.vector.scalar_tensor_tensor(out=max_rows[:, 1], in0=aux_ps[0:MAXES // HALVES, bank, 0:P],
                                               scalar=1.0 / MAX_LIFT, in1=max_rows[:, 0], op0=ALU.mult,
                                               op1=ALU.subtract).then_inc(rows_split, 1)

            def invert(n, half, piece):
                h = n * HALVES + half
                dve.wait_ge(weighed, (h + 1) * KEY_TILES)
                need(dve, z_made, h - 1)
                at = slice(piece * CHUNK // PIECES, (piece + 1) * CHUNK // PIECES)
                nc.vector.reciprocal(recip[:, half, at], sum_ps[:, at]).then_inc(recip_made, 1)

            def make_z(n, half):
                h = n * HALVES + half
                dve.wait_ge(recip_made, (h + 1) * PIECES)
                dve.wait_ge(mix_kept, h + 1)
                need(dve, z_split, h - 1)
                nc.vector.scalar_tensor_tensor(out=z[:, half], in0=mixed[:, half], scalar=QUERY_LIFT,
                                               in1=recip[:, half], op0=ALU.mult, op1=ALU.mult).then_inc(z_made, 1)

            def normalise(b, u, tt):
                dve.wait_ge(rstd_made, b * HALVES + u + 1)
                nc.vector.tensor_scalar(total[:, u, tt], total[:, u, tt], moments[:, u, tt, 0:1],
                                        rstd[:, u, tt:tt + 1], ALU.subtract, ALU.mult).then_inc(normed, 1)

            for i, tile_before in enumerate(before_all):
                aux(*tile_before, (i + 1) % 2)
            combine(0)
            max_rows_low(0, len(before_all) % 2)

            def body(b):
                for g in range(GROUPS):
                    n = b * GROUPS + g
                    work = unit_work(b, g)
                    position = 0
                    for unit in range(LEAD, UNITS):
                        if unit == (1 if g == 0 else 2) and not (is_first(b) and g == 0):
                            for piece in range(PIECES):
                                invert(n - 1, 1, piece)
                            make_z(n - 1, 1)
                        if HALF_UNITS + 2 <= unit < HALF_UNITS + 2 + PIECES:
                            invert(n, 0, unit - HALF_UNITS - 2)
                        if unit == HALF_UNITS + 2 + PIECES:
                            make_z(n, 0)
                        for kind, t in work[unit]:
                            aux(b, g, n, kind, t, (g + position) % 2)
                            position += 1
                        if g == 0 and not is_first(b) and 11 <= unit < 11 + TILES:
                            normalise(b - 1, (unit - 11) // TT, (unit - 11) % TT)
                    if not (is_last(b) and g == GROUPS - 1):
                        combine(n + 1)
                        max_rows_low(n + 1, (g + position) % 2)

            over_batches(dve, body)
            for piece in range(PIECES):
                invert(STEPS - 1, 1, piece)
            make_z(STEPS - 1, 1)
            for t in range(TILES):
                aux(BATCH, 0, 0, "o", t, (t + 1) % 2)
            for t in range(TILES):
                normalise(BATCH - 1, t // TT, t % TT)

        @block.tensor
        def _(pe):
            FIRST_TILES = 1
            PRODUCTS = ((0, 0), (0, 1), (1, 0))
            w_parts, x_parts, z_parts = (w_hi, w_lo), (x_hi, x_lo), (z_hi, z_lo)

            def wait_taken(b, g, n, kind, t):
                if kind == "t":
                    pe.wait_ge(x_split, (b + 1) * 2 * KT + t + 1)
                elif kind == "v":
                    pe.wait_ge(v_made, b * TILES + t + 1)
                elif kind == "o":
                    pe.wait_ge(residual, (b - 1) * TILES + t + 1)
                elif kind == "q":
                    pe.wait_ge(qk_full_made, 4 * (n + 2) + t + 1)
                elif kind == "m":
                    pe.wait_ge(maxed, (n + 1) * MAXES + t + 1)
                elif kind == "r":
                    pe.wait_ge(rows_split, n + 2)

            def tile(b, g, n, kind, t, bank):
                if kind == "t":
                    half, k = t // KT, t % KT
                    pe.wait_ge(rows_loaded[half], 16 * (b + 2))
                    for tt in range(TT):
                        last = nc.tensor.transpose(aux_ps[:, bank, tt * P:(tt + 1) * P],
                                                   x_tok[:, half, tt, k * P:(k + 1) * P], ident)
                    last.then_inc(x_turned, 1)
                elif kind == "q":
                    which, half = t // 2, t % 2
                    group = (g + 2) % GROUPS
                    pe.wait_ge(x_split, (b + 1 if g < 2 else b + 2) * 2 * KT)
                    for k in range(KT):
                        for i, (a, c) in enumerate(PRODUCTS):
                            last = nc.tensor.matmul(aux_ps[:, bank], w_parts[a][:, which, k, group * P:(group + 1) * P],
                                                    x_parts[c][:, k, half * CHUNK:(half + 1) * CHUNK],
                                                    start=(k == 0 and i == 0), stop=(k == KT - 1 and i == 2))
                    last.then_inc(qk_ready, 1)
                elif kind in ("v", "o"):
                    if kind == "v":
                        parts, which, done = x_parts, WV, v_ready
                        pe.wait_ge(x_split, (b + 1) * 2 * KT)
                    else:
                        parts, which, done = z_parts, WO, o_ready
                        pe.wait_ge(z_split, b * GROUPS * HALVES)
                    for k in range(KT):
                        for i, (a, c) in enumerate(PRODUCTS):
                            last = nc.tensor.matmul(aux_ps[:, bank], parts[c][:, k, t * P:(t + 1) * P],
                                                    w_parts[a][:, which, k], start=(k == 0 and i == 0),
                                                    stop=(k == KT - 1 and i == 2))
                    last.then_inc(done, 1)
                elif kind == "m":
                    j, qt, kh = t // (KEY_TILES * HALVES), t // HALVES % KEY_TILES, t % HALVES
                    buffer = (g + 1) % 2
                    if t == 0:
                        pe.wait_ge(stacked[buffer], (b * 2 + (g + 1) // 2 + 1) * STACK_DMAS * 16)
                    last = nc.tensor.matmul(aux_ps[:, bank], queries[0:3 * HEAD, buffer, j, qt * P:(qt + 1) * P],
                                            keys[0:3 * HEAD, buffer, j, kh * CHUNK:(kh + 1) * CHUNK],
                                            start=True, stop=True)
                    last.then_inc(m_ready, 1)
                elif kind == "r":
                    pe.wait_ge(row_max_made, n + 2)
                    nc.tensor.transpose(aux_ps[0:MAXES // HALVES, bank, 0:P], row_max[:], ident).then_inc(rows_turned, 1)

            held = [None, None]

            def aux(b, g, n, kind, t, bank):
                if held[bank]:
                    wait_taken(*held[bank])
                held[bank] = (b, g, n, kind, t)
                tile(b, g, n, kind, t, bank)

            def scores(n, g, unit):
                half, kt, pair = unit // HALF_UNITS, (unit % HALF_UNITS) // 2, unit % 2
                buffer = g % 2
                if unit == 0:
                    pe.wait_ge(rows_stacked, 32 * (n + 1))
                need(pe, exp_made, n * UNITS + unit - 1)
                for i in range(PAIR):
                    j = PAIR * pair + i
                    last = nc.tensor.matmul(score_ps[:, unit % 2, i], keys[:, buffer, j, kt * P:(kt + 1) * P],
                                            queries[:, buffer, j, half * CHUNK:(half + 1) * CHUNK],
                                            start=True, stop=True)
                last.then_inc(scored, 1)

            def weigh(b, n, g, half, kt):
                pe.wait_ge(exp_made, n * UNITS + half * HALF_UNITS + 2 * kt + 2)
                if g == 0 and half == 0 and kt == 0:
                    pe.wait_ge(v_made, (b + 1) * TILES)
                if kt == 0:
                    need(pe, mix_kept, n * HALVES + half)
                for j in range(G_HEADS):
                    slot = (2 * kt + j // PAIR) % PROBS
                    last = nc.tensor.matmul(mix_ps[j * HEAD:(j + 1) * HEAD, :],
                                            v[:, kt, (G_HEADS * g + j) * HEAD:(G_HEADS * g + j + 1) * HEAD],
                                            probs[:, slot, j % PAIR], start=(kt == 0), stop=(kt == KEY_TILES - 1))
                if kt < POOLED:
                    last.then_inc(weighed, 1)

            def sum_up(n, half, kt):
                if kt == POOLED:
                    h = n * HALVES + half
                    pe.wait_ge(pooled, (h + 1) * 2 * (POOLED - 1))
                    need(pe, recip_made, h * PIECES)
                    for j in range(G_HEADS):
                        nc.tensor.matmul(sum_ps[j * HEAD:(j + 1) * HEAD, :], ones[:, 0:HEAD], prob_sums[:, j],
                                         start=True, stop=False)
                for j in range(G_HEADS):
                    slot = (2 * kt + j // PAIR) % PROBS
                    last = nc.tensor.matmul(sum_ps[j * HEAD:(j + 1) * HEAD, :], ones[:, 0:HEAD],
                                            probs[:, slot, j % PAIR], start=False, stop=(kt == KEY_TILES - 1))
                last.then_inc(weighed, 1)

            for i, tile_before in enumerate(before_all):
                aux(*tile_before, (i + 1) % 2)

            def body(b):
                before = b * GROUPS - 1
                held[:] = [(b - 1, GROUPS - 1, before, "m", MAXES - 1), (b - 1, GROUPS - 1, before, "r", 0)]
                for g in range(GROUPS):
                    n = b * GROUPS + g
                    work = unit_work(b, g)
                    position = 0
                    for unit in range(LEAD, UNITS):
                        if unit != LEAD:
                            scores(n, g, unit)
                        tile_before = unit // 2 - 1
                        weighing = unit >= 3 and unit % 2 == 1
                        for place, (kind, t) in enumerate(work[unit]):
                            if weighing and place == FIRST_TILES:
                                weigh(b, n, g, tile_before // KEY_TILES, tile_before % KEY_TILES)
                            if weighing and place == FIRST_TILES + 2 and tile_before % KEY_TILES >= POOLED:
                                sum_up(n, tile_before // KEY_TILES, tile_before % KEY_TILES)
                            aux(b, g, n, kind, t, (g + position) % 2)
                            position += 1
                        if weighing and len(work[unit]) <= FIRST_TILES:
                            weigh(b, n, g, tile_before // KEY_TILES, tile_before % KEY_TILES)
                        if weighing and len(work[unit]) <= FIRST_TILES + 2 and tile_before % KEY_TILES >= POOLED:
                            sum_up(n, tile_before // KEY_TILES, tile_before % KEY_TILES)
                    if not (is_last(b) and g == GROUPS - 1):
                        aux(b, g, n, "r", 0, (g + position) % 2)
                    weigh(b, n, g, 1, KEY_TILES - 1)
                    sum_up(n, 1, KEY_TILES - 1)

            pe.wait_ge(key_ones_set, 1)
            over_batches(pe, body)
            for t in range(TILES):
                aux(BATCH, 0, STEPS, "o", t, (t + 1) % 2)


def build(nc, args, out):
    between = [nc.dram_tensor("after_stage%d" % n, (TOKENS, D), F32, kind="Internal").ap() for n in range(3)]
    ternary = [nc.dram_tensor("ternary_w%d" % (n + 1), (P, args["L1_ffn_w1"].shape[1] * KT), F16, kind="Internal").ap()
               for n in range(3)]
    with ExitStack() as stack:
        ident = stack.enter_context(nc.sbuf_tensor("ident", [P, P], F32))
        ones = stack.enter_context(nc.sbuf_tensor("ones", [P, P], F32))
        setup_constants(nc, ident, ones)
        retention_phase(nc, args["L0_attn_x"], args["L0_attn_x_T"], between[0], ident[:],
                        [args["L0_attn_" + n] for n in ("Wv", "Wq", "Wg", "Wo")],
                        args["L0_attn_beta"], args["L0_attn_ln_w"], args["L0_attn_ln_b"])
        quantized_ffn_stage(nc, args, ident, between[0], between[1], ternary)
        attention_stage(nc, args, ident, ones, between[1], between[2])
        ternary_ffn_stage(nc, args, ident, ternary, between[2], out)


def quantized_ffn_stage(nc, args, ident, x_in, x_out, ternary):
    hidden_tiles = args["L0_ffn_gate_w"].shape[1] // P
    with ExitStack() as stack:
        gate_scale = stack.enter_context(nc.sbuf_tensor("gate_scale", [P, hidden_tiles], F32))
        up_scale = stack.enter_context(nc.sbuf_tensor("up_scale", [P, hidden_tiles], F32))
        down_scale = stack.enter_context(nc.sbuf_tensor("down_scale", [P, D], F32))
        w_gate = stack.enter_context(nc.sbuf_tensor("w_gate", [P, KT, hidden_tiles * P], F16))
        w_up = stack.enter_context(nc.sbuf_tensor("w_up", [P, KT, hidden_tiles * P], F16))
        w_down = stack.enter_context(nc.sbuf_tensor("w_down", [P, hidden_tiles, D], F32R))
        fp8_weights(nc, (args["L0_ffn_gate_w"], args["L0_ffn_up_w"], args["L0_ffn_down_w"]), (w_gate, w_up, w_down),
                    [(args["L0_ffn_gate_scale"], gate_scale), (args["L0_ffn_up_scale"], up_scale)],
                    [(args["L0_ffn_down_scale"], down_scale)])
        sums = nc.dram_tensor("ternary_partition_sums", (P, len(ternary)), F32, kind="Internal").ap()
        beside = TernaryWeights(nc, stack, [args["L1_ffn_w%d" % n] for n in (1, 2, 3)], ternary, sums)
        ffn_phase(nc, "ffn0_", x_in, x_out, ident[:], w_gate, w_up, w_down, hidden_tiles, ACT.Silu,
                  gate_scale[:], up_scale[:], down_scale[:], F32R, beside)


def attention_stage(nc, args, ident, ones, x_in, x_out):
    with ExitStack() as stack:
        w_hi = stack.enter_context(nc.sbuf_tensor("att_w_hi", [P, 4, KT, D], F16))
        w_lo = stack.enter_context(nc.sbuf_tensor("att_w_lo", [P, 4, KT, D], F16))
        bias_cols = stack.enter_context(nc.sbuf_tensor("att_bias_cols", [P, 2, KT], F32))
        bias_rows = stack.enter_context(nc.sbuf_tensor("att_bias_rows", [P, 2, D], F32))
        exp_scale = stack.enter_context(nc.sbuf_tensor("att_exp_scale", [P, 1], F32))
        out_scale = stack.enter_context(nc.sbuf_tensor("att_out_scale", [P, 1], F32))
        names = ("q", "k", "v", "o")
        lora_weights(nc, ident[:], [args["L1_attn_W" + n] for n in names], [args["L1_attn_A" + n] for n in names],
                     [args["L1_attn_B" + n] for n in names], [args["L1_attn_b" + n] for n in names],
                     w_hi, w_lo, bias_cols, bias_rows, exp_scale, out_scale)
        attention_phase(nc, x_in, x_out, ident[:], ones, w_hi, w_lo, bias_cols, bias_rows, exp_scale, out_scale)


def ternary_ffn_stage(nc, args, ident, ternary, x_in, x_out):
    hidden_tiles = args["L1_ffn_w1"].shape[1] // P
    with ExitStack() as stack:
        w1 = stack.enter_context(nc.sbuf_tensor("w1", [P, KT, hidden_tiles * P], F16))
        w2 = stack.enter_context(nc.sbuf_tensor("w2", [P, KT, hidden_tiles * P], F16))
        w3 = stack.enter_context(nc.sbuf_tensor("w3", [P, hidden_tiles, D], F16))
        ffn_phase(nc, "ffn1_", x_in, x_out, ident[:], w1, w2, w3, hidden_tiles, ACT.Sigmoid,
                  None, None, None, F16, weight_sources=ternary)


_TRANSPOSED = ('L0_attn_Wq', 'L0_attn_Wv', 'L0_attn_Wg', 'L0_attn_Wo', 'L1_attn_Wq', 'L1_attn_Wk', 'L1_attn_Wv',
               'L1_attn_Wo', 'L1_attn_Aq', 'L1_attn_Ak', 'L1_attn_Av', 'L1_attn_Ao', 'L1_ffn_w1', 'L1_ffn_w2',
               'L1_ffn_w3')


def kernel(**inputs):
    import numpy as _np
    import concourse.bacc as _bacc
    from concourse import mybir as _mybir
    from concourse.bass_utils import run_bass_kernel_spmd as _run

    nc = _bacc.Bacc("TRN2", target_bir_lowering=False, num_devices=1)
    arrays, args = {}, {}

    def give(name, array):
        a = _np.ascontiguousarray(array)
        arrays[f"in_{name}"] = a
        args[name] = nc.dram_tensor(f"in_{name}", a.shape, _mybir.dt.from_np(a.dtype), kind="ExternalInput").ap()

    for name, value in inputs.items():
        a = _np.asarray(value)
        if name == 'L0_attn_x':
            rows = a.reshape(-1, a.shape[-1])
            give(name, rows)
            give(name + "_T", rows.T)
        else:
            give(name, a.T if name in _TRANSPOSED else a)
    shape = _np.asarray(inputs['L0_attn_x']).shape
    out = nc.dram_tensor("out", (shape[0] * shape[1], shape[2]), _mybir.dt.float32, kind="ExternalOutput").ap()
    build(nc, args, out)
    r = _run(nc, [arrays], core_ids=[0])
    return r.results[0]["out"].reshape(shape)
```
